# Optimizing a Trainium2 kernel written in Bass

```python
import numpy as np
import jax
import jax.numpy as jnp

def _softmax(x, axis=-1):
    return jax.nn.softmax(x, axis=axis)

def _gelu(x):
    return jax.nn.gelu(x, approximate=True)

def _silu(x):
    return jax.nn.silu(x)

def _sigmoid(x):
    return jax.nn.sigmoid(x)

def _layernorm(x, axis=-1, eps=1e-05):
    m = jnp.mean(x, axis=axis, keepdims=True)
    v = jnp.var(x, axis=axis, keepdims=True)
    return (x - m) / jnp.sqrt(v + eps)

def _scatter_add(tgt, idx, src, axis=0):
    return tgt.at[idx].add(src)

def _segment_sum(src, seg, n):
    return jax.ops.segment_sum(src, seg, n)
kernel_name = 'mk_xattn_ffn_d1_seqx_r4_735e3a'

def setup_inputs(seed: int=0):
    np.random.seed(seed)
    _w = jnp.asarray

    def _rec_inputs():
        import jax
        import jax.numpy as jnp
        _rk = jax.random.key(seed)
        x = 0.0002417 + 0.9998 * jax.random.normal(jax.random.fold_in(_rk, 1), (64, 128, 256), jnp.float32)
        _lenS = 128 - jax.random.randint(jax.random.fold_in(_rk, 7), (64,), 0, max(1, 128 // 4) + 1, jnp.int32)
        _lenS2 = 128 - jax.random.randint(jax.random.fold_in(_rk, 8), (64,), 0, max(1, 128 // 4) + 1, jnp.int32)
        _ctx_1024P = jax.random.normal(jax.random.fold_in(_rk, 11), (64, 16, 256), jnp.float32)
        _ctx_1024c = jax.random.dirichlet(jax.random.fold_in(_rk, 511), 0.3 * jnp.ones((16,), jnp.float32), (64, 128))
        _ctx_1024t = jnp.einsum('bsk,bkd->bsd', _ctx_1024c, _ctx_1024P)
        _ctx_1024t = _ctx_1024t * jax.lax.rsqrt(jnp.mean(jnp.square(_ctx_1024t)) + 1e-12) * 0.953939
        ctx_1024 = 7.22013e-05 + 1.00017 * (_ctx_1024t + 0.3 * jax.random.normal(jax.random.fold_in(_rk, 611), (64, 128, 256), jnp.float32))
        _validS = jnp.arange(128)[None, :] < _lenS[:, None]
        _validS2 = jnp.arange(128)[None, :] < _lenS2[:, None]
        _causal = jnp.tril(jnp.ones((128, 128), dtype=bool))
        mask_Bx1x1xS2_if1 = jnp.where(jnp.ones((64, 1, 1, 128), dtype=bool), 1, 0).astype(jnp.int32)
        return (x, ctx_1024, mask_Bx1x1xS2_if1)
    x, ctx_1024, mask_Bx1x1xS2_if1 = _rec_inputs()

    def _L0_xattn_setup():
        import jax, jax.numpy as jnp
        import numpy as np
        EMBED = 256
        HEADS = 16
        HEAD_DIM = EMBED // HEADS
        key = jax.random.key(seed)
        ks = jax.random.split(key, 12)
        N, L, E = (4, 512, EMBED)
        s = 1.0 / np.sqrt(E)
        return {'values': jax.random.normal(ks[0], (N, L, E), jnp.float32), 'keys': jax.random.normal(ks[1], (N, L, E), jnp.float32), 'query': jax.random.normal(ks[2], (N, L, E), jnp.float32), 'mask': jnp.ones((N, 1, 1, L), jnp.int32), 'Wv': jax.random.normal(ks[3], (E, E), jnp.float32) * s, 'bv': jnp.zeros((E,), jnp.float32), 'Wk': jax.random.normal(ks[4], (E, E), jnp.float32) * s, 'bk': jnp.zeros((E,), jnp.float32), 'Wq': jax.random.normal(ks[5], (E, E), jnp.float32) * s, 'bq': jnp.zeros((E,), jnp.float32), 'Wo': jax.random.normal(ks[6], (E, E), jnp.float32) * s, 'bo': jnp.zeros((E,), jnp.float32)}
    _L0_xattn_all = _L0_xattn_setup()
    _L0_xattn_in = {k: v for k, v in _L0_xattn_all.items() if k in ('Wv', 'bv', 'Wk', 'bk', 'Wq', 'bq', 'Wo', 'bo')}
    del _L0_xattn_all

    def _L0_ffn_setup():
        import jax, jax.numpy as jnp
        import numpy as np
        HIDDEN = 256
        INTER = 1024
        key = jax.random.key(seed)
        k1, k2, k3, k4, k5 = jax.random.split(key, 5)
        hidden_states = jax.random.normal(k1, (4, 512, HIDDEN), dtype=jnp.float32)
        W1 = jax.random.normal(k2, (HIDDEN, INTER), dtype=jnp.float32) * (1.0 / np.sqrt(HIDDEN))
        b1 = jax.random.normal(k3, (INTER,), dtype=jnp.float32) * 0.02
        W2 = jax.random.normal(k4, (INTER, HIDDEN), dtype=jnp.float32) * (1.0 / np.sqrt(INTER))
        b2 = jax.random.normal(k5, (HIDDEN,), dtype=jnp.float32) * 0.02
        return {'hidden_states': hidden_states, 'W1': W1, 'b1': b1, 'W2': W2, 'b2': b2}
    _L0_ffn_all = _L0_ffn_setup()
    _L0_ffn_in = {k: v for k, v in _L0_ffn_all.items() if k in ('W1', 'b1', 'W2', 'b2')}
    del _L0_ffn_all
    return {'x': x, 'ctx_1024': ctx_1024, 'mask_Bx1x1xS2_if1': mask_Bx1x1xS2_if1, 'L0_xattn_Wv': _L0_xattn_in['Wv'], 'L0_xattn_bv': _L0_xattn_in['bv'], 'L0_xattn_Wk': _L0_xattn_in['Wk'], 'L0_xattn_bk': _L0_xattn_in['bk'], 'L0_xattn_Wq': _L0_xattn_in['Wq'], 'L0_xattn_bq': _L0_xattn_in['bq'], 'L0_xattn_Wo': _L0_xattn_in['Wo'], 'L0_xattn_bo': _L0_xattn_in['bo'], 'L0_ffn_W1': _L0_ffn_in['W1'], 'L0_ffn_b1': _L0_ffn_in['b1'], 'L0_ffn_W2': _L0_ffn_in['W2'], 'L0_ffn_b2': _L0_ffn_in['b2']}

def reference(x, ctx_1024, mask_Bx1x1xS2_if1, L0_xattn_Wv, L0_xattn_bv, L0_xattn_Wk, L0_xattn_bk, L0_xattn_Wq, L0_xattn_bq, L0_xattn_Wo, L0_xattn_bo, L0_ffn_W1, L0_ffn_b1, L0_ffn_W2, L0_ffn_b2):
    import jax
    import jax.numpy as jnp

    def _L0_xattn_ref(values, keys, query, mask, Wv, bv, Wk, bk, Wq, bq, Wo, bo):
        import jax, jax.numpy as jnp
        import numpy as np
        EMBED = 256
        HEADS = 16
        HEAD_DIM = EMBED // HEADS
        N, L, E = values.shape
        H, D = (HEADS, HEAD_DIM)
        v = (values @ Wv + bv).reshape(N, L, H, D)
        k = (keys @ Wk + bk).reshape(N, L, H, D)
        q = (query @ Wq + bq).reshape(N, L, H, D)
        energy = jnp.einsum('nqhd,nkhd->nhqk', q, k)
        energy = jnp.where(mask == 0, jnp.float32(-1e+20), energy)
        attn = jax.nn.softmax(energy / np.sqrt(D), axis=3)
        out = jnp.einsum('nhqk,nkhd->nqhd', attn, v).reshape(N, L, E)
        return out @ Wo + bo

    def _L0_ffn_ref(hidden_states, W1, b1, W2, b2):
        import jax, jax.numpy as jnp
        import numpy as np
        HIDDEN = 256
        INTER = 1024
        h = jax.nn.relu(jnp.einsum('bsh,hi->bsi', hidden_states, W1) + b1)
        return jnp.einsum('bsi,ih->bsh', h, W2) + b2
    x = x + _L0_xattn_ref(ctx_1024, ctx_1024, _layernorm(x, axis=-1), mask_Bx1x1xS2_if1, L0_xattn_Wv, L0_xattn_bv, L0_xattn_Wk, L0_xattn_bk, L0_xattn_Wq, L0_xattn_bq, L0_xattn_Wo, L0_xattn_bo)
    x = x + _L0_ffn_ref(_layernorm(x, axis=-1), L0_ffn_W1, L0_ffn_b1, L0_ffn_W2, L0_ffn_b2)
    return x

_drawn_inputs = setup_inputs


def setup_inputs(seed=0):
    import zlib

    import numpy as np

    out = dict(_drawn_inputs(seed))
    spreads = {'L0_xattn_bv': (0.0, 0.1),
     'L0_xattn_bk': (0.0, 0.8),
     'L0_xattn_bq': (0.0, 0.377),
     'L0_xattn_bo': (0.0, 0.1)}
    factors = {'L0_ffn_b1': 5.457, 'L0_ffn_b2': 3.912}
    for name, (base, spread) in spreads.items():
        noise = np.random.default_rng([zlib.crc32(name.encode()), seed]).standard_normal(out[name].shape)
        drawn = base * np.exp(spread * noise) if base else spread * noise
        out[name] = jnp.asarray(drawn.astype(out[name].dtype))
    for name, factor in factors.items():
        out[name] = (out[name] * factor).astype(out[name].dtype)
    return out
```

```python
import numpy as np
import concourse.bass as bass
from concourse import mybir
from contextlib import ExitStack


B, S, E, HEADS, F = 64, 128, 256, 16, 1024
D = E // HEADS
P = 128
GB = 2
T = GB * S
GROUPS = B // GB
KT = E // P
FT = F // P
HH = P // D
QUADS = HEADS // 4
EPS = 1e-5
MASKED = float(np.float32(-1e20))
SCORE_SCALE = 1.0 / float(np.sqrt(D))
PAIRS = ((0, 0), (0, 1), (1, 0), (0, 2), (1, 1), (2, 0))
ROWS_PRODUCTS = len(PAIRS) * D
ROWS_MASK = ROWS_PRODUCTS + 3
ROWS_MAX = ROWS_MASK + 3


def stage_lags():
    return {"N": 0, "A": 1, "B": 2, "C": 3, "F": 4}


LAG = stage_lags()


class Step:

    def __init__(self, pair, k, in_loop):
        self.pair, self.k, self.in_loop = pair, k, in_loop

    def has(self, stage):
        return self.in_loop or 0 <= self.k - LAG[stage] < GROUPS

    def before(self):
        return Step(self.pair, self.k - 1, self.in_loop)

    def parity(self, stage):
        return (self.k - LAG[stage]) % 2

    def group(self, stage):
        return self.pair * 2 + (self.k - LAG[stage])

    def count(self, stage, per, done):
        return self.pair * (2 * per) + (per * (self.k - LAG[stage]) + done)

    def count_alternate(self, stage, per, done):
        return self.pair * per + (per * ((self.k - LAG[stage]) // 2) + done)


def split3(value):
    parts, rest = [], np.float32(value)
    for _ in range(3):
        bits = np.array(rest, np.float32).view(np.uint32).astype(np.uint64)
        bits = ((bits + 0x7FFF + ((bits >> 16) & 1)) & 0xFFFF0000).astype(np.uint32)
        part = bits.view(np.float32)
        parts.append(float(part))
        rest = np.float32(rest - part)
    return parts


def build(nc, x, ctx_t, mask, wq, wk, wv, wo, w1, w2, bq, bk, bv, bo, b1, b2, out):
    fp32, f32r, bf16, i32 = mybir.dt.float32, mybir.dt.float32r, mybir.dt.bfloat16, mybir.dt.int32
    ALU, ACT, AX = mybir.AluOpType, mybir.ActivationFunctionType, mybir.AxisListType

    x_g = x.rearrange("(g j) p e -> g p j e", j=GB)
    out_g = out.rearrange("(g j) p e -> g p j e", j=GB)
    mask_g = mask.rearrange("(g j) a b k -> g (a b) (j k)", j=GB)

    ctx = ExitStack()
    with ctx:
        def sb(name, shape, dt=fp32):
            return ctx.enter_context(nc.sbuf_tensor(name, shape, dt))

        def sem(name):
            return ctx.enter_context(nc.semaphore(name))

        w_cols = {"wq": KT * E, "wk": KT * E, "wv": KT * E, "wo": KT * E, "w1": KT * F, "w2": FT * E}
        w_raw = sb("w_raw", [P, sum(w_cols.values())])
        w_hi = {n: sb(f"{n}_hi", [P, c], f32r) for n, c in w_cols.items()}
        w_lo = {n: sb(f"{n}_lo", [P, c], f32r) for n, c in w_cols.items()}
        bq_col, bk_col, b1_col = sb("bq_col", [P, KT]), sb("bk_col", [P, KT]), sb("b1_col", [P, FT])
        bv_row, bo_row, b2_row = sb("bv_row", [P, 1, E]), sb("bo_row", [P, 1, E]), sb("b2_row", [P, 1, E])
        ident = sb("ident", [P, P])
        ident_bf = sb("ident_bf", [P, P], bf16)
        minus_half = sb("minus_half", [P, GB])

        x_in = [sb(f"x_in{i}", [P, GB, E]) for i in range(2)]
        n_stats, n_mv = sb("n_stats", [P, GB, 6]), sb("n_mv", [P, GB, 2])
        n_var, n_rstd = sb("n_var", [P, GB]), sb("n_rstd", [P, GB])
        xn = sb("xn", [P, GB, E])
        ctx_in = [sb(f"ctx_in{i}", [P, KT, T]) for i in range(2)]
        mask_in = [sb(f"mask_in{i}", [P, T], i32) for i in range(2)]
        keep = sb("keep", [P, T])
        mask_parts = sb("mask_parts", [1, 3, T], bf16)
        ctx_hi, ctx_lo = sb("ctx_hi", [P, KT, T], f32r), sb("ctx_lo", [P, KT, T], f32r)
        xnT_hi, xnT_lo = sb("xnT_hi", [P, KT, T], f32r), sb("xnT_lo", [P, KT, T], f32r)
        q_rest, k_rest = sb("q_rest", [P, KT, T]), sb("k_rest", [P, KT, T])
        q_parts, k_parts = sb("q_parts", [P, 3, KT, T], bf16), sb("k_parts", [P, 3, KT, T], bf16)
        q_rows = [sb(f"q_rows{i}", [P, HEADS, T], bf16) for i in range(2)]
        k_rows = [sb(f"k_rows{i}", [P, HEADS, T], bf16) for i in range(2)]
        v_ones = [sb(f"v_ones{i}", [P, GB, HEADS, 2 * D]) for i in range(2)]
        minus_max, max_rest = sb("minus_max", [P, HEADS]), sb("max_rest", [P, HEADS])
        max_parts = sb("max_parts", [P, 3, HEADS], bf16)
        max_rows = sb("max_rows", [3 * HEADS, S], bf16)
        probs = sb("probs", [P, HEADS, S])
        attn_raw = sb("attn_raw", [P, QUADS, T])
        numer, denom = sb("numer", [P, KT, T]), sb("denom", [P, KT, T])
        attn_hi, attn_lo = sb("attn_hi", [P, KT, T], f32r), sb("attn_lo", [P, KT, T], f32r)
        x_res, x2, x2_bias = sb("x_res", [P, GB, E]), sb("x2", [P, GB, E]), sb("x2_bias", [P, GB, E])
        c_stats, c_mv = sb("c_stats", [P, GB, 6]), sb("c_mv", [P, GB, 2])
        c_var, c_rstd = sb("c_var", [P, GB]), sb("c_rstd", [P, GB])
        x2n = sb("x2n", [P, GB, E])
        x2T_hi, x2T_lo = sb("x2T_hi", [P, KT, T], f32r), sb("x2T_lo", [P, KT, T], f32r)
        hid = [sb(f"hid{i}", [P, 2, T]) for i in range(2)]
        hid_hi, hid_lo = sb("hid_hi", [P, FT, T], f32r), sb("hid_lo", [P, FT, T], f32r)

        scores = [ctx.enter_context(nc.psum_tensor(f"scores{i}", [P, HEADS // 2, S], fp32)) for i in range(2)]
        attn_ps = ctx.enter_context(nc.psum_tensor("attn_ps", [P, QUADS, S], fp32))
        bank = {n: ctx.enter_context(nc.psum_tensor(f"bank_{n}", [P, 2, T], fp32)) for n in "ABC"}
        max_ps = attn_ps[:, :, :].rearrange("p a b -> p (a b)").bitcast(bf16)[0:3 * HEADS, 0:S]

        w_loaded, consts_loaded, w_split_hi, w_split = sem("w_loaded"), sem("consts_loaded"), sem("w_split_hi"), sem("w_split")
        ident_zeroed, consts_set = sem("ident_zeroed"), sem("consts_set")
        x_loaded, ctx_loaded = [sem("x_loaded0"), sem("x_loaded1")], [sem("ctx_loaded0"), sem("ctx_loaded1")]
        mask_loaded = [sem("mask_loaded0"), sem("mask_loaded1")]
        res_loaded, out_stored = sem("res_loaded"), sem("out_stored")
        n_bn, n_ag, n_var_done, n_pow = sem("n_bn"), sem("n_ag"), sem("n_var_done"), sem("n_pow")
        xn_done, xnT_mm, xnT_hi_done, xnT_lo_done = sem("xn_done"), sem("xnT_mm"), sem("xnT_hi_done"), sem("xnT_lo_done")
        keep_done, mask_parts_done = sem("keep_done"), sem("mask_parts_done")
        ctx_hi_done, ctx_lo_done = sem("ctx_hi_done"), sem("ctx_lo_done")
        q_mm, k_mm, v_mm = sem("q_mm"), sem("k_mm"), sem("v_mm")
        q_out, k_out, q_hi_done, k_hi_done = sem("q_out"), sem("k_out"), sem("q_hi_done"), sem("k_hi_done")
        q_split, k_split, v_done = sem("q_split"), sem("k_split"), sem("v_done")
        q_rows_in, k_rows_in = [sem("q_rows_in0"), sem("q_rows_in1")], [sem("k_rows_in0"), sem("k_rows_in1")]
        scores_mm, max_done, max_split, maxT_mm, max_rows_done = sem("scores_mm"), sem("max_done"), sem("max_split"), sem("maxT_mm"), sem("max_rows_done")
        max_rows_in, shifted_mm, probs_done, attn_mm, attn_out = sem("max_rows_in"), sem("shifted_mm"), sem("probs_done"), sem("attn_mm"), sem("attn_out")
        packed = sem("packed")
        recip_done, attn_norm, attn_split, o_mm = sem("recip_done"), sem("attn_norm"), sem("attn_split"), sem("o_mm")
        res_bias, x2_done, x2_bias_done = sem("res_bias"), sem("x2_done"), sem("x2_bias_done")
        c_bn, c_ag, c_var_done, c_pow = sem("c_bn"), sem("c_ag"), sem("c_var_done"), sem("c_pow")
        x2n_done, x2T_mm, x2T_hi_done, x2T_lo_done = sem("x2n_done"), sem("x2T_mm"), sem("x2T_hi_done"), sem("x2T_lo_done")
        hid_mm, hid_out, hid_hi_done, hid_lo_done = sem("hid_mm"), sem("hid_out"), sem("hid_hi_done"), sem("hid_lo_done")
        f_mm, y_done = sem("f_mm"), sem("y_done")
        act_passed, sp_passed, pool_passed, dve_passed, pe_passed = sem("act_passed"), sem("sp_passed"), sem("pool_passed"), sem("dve_passed"), sem("pe_passed")

        def alone(eng, passed, semaphore, value):
            if isinstance(value, int):
                if value > 0:
                    eng.wait_ge(semaphore, value)
            else:
                eng.wait_ge(semaphore, value)
                eng.sem_inc(passed, 1)

        FILLS = [("xnT", "A", "C", xnT_lo_done, 1), ("q", "A", "B", q_out, 1), ("f", "F", "A", y_done, 1),
                 ("k", "A", "C", k_out, 1), ("o", "C", "B", x2_done, 1), ("v", "A", "C", v_done, 1),
                 ("x2T", "C", "A", x2T_lo_done, 1), ("h0", "C", "B", hid_out, 4), ("h1", "C", "C", hid_out, 4),
                 ("h2", "C", "A", hid_out, 4), ("h3", "C", "B", hid_out, 4)]

        def bank_free(eng, st, name):
            names = [f[0] for f in FILLS]
            me = FILLS[names.index(name)]
            here = [(st, f) for f in FILLS[:names.index(name)] if f[2] == me[2] and st.has(f[1])]
            prev, back = st, []
            while not here and not back:
                prev = prev.before()
                if not prev.in_loop and prev.k < 0:
                    return
                back = [(prev, f) for f in FILLS if f[2] == me[2] and prev.has(f[1])]
            at, f = (here or back)[-1]
            done = 1 if f[4] == 1 else int(f[0][1:]) + 1
            eng.wait_ge(f[3], at.count(f[1], f[4], done))

        def over_steps(eng, run_step):
            full = LAG["F"]
            for k in range(full):
                run_step(Step(0, k, False))
            with eng.Fori(0, (GROUPS - full) // 2) as pair:
                run_step(Step(pair, full, True))
                run_step(Step(pair, full + 1, True))
            for k in range(GROUPS, GROUPS + full):
                run_step(Step(0, k, False))

        block = ctx.enter_context(nc.Block())

        @block.sync
        def _(sp):
            def load_group(st):
                group, par = st.group("N"), st.parity("N")
                if st.in_loop or st.k > 1:
                    alone(sp, sp_passed, xn_done, st.count("A", GB, 0))
                    alone(sp, sp_passed, ctx_lo_done, st.count("A", 1, 0))
                    alone(sp, sp_passed, keep_done, st.count("A", 1, 0))
                    alone(sp, sp_passed, mask_parts_done, st.count("A", 1, 0))
                sp.dma_start(x_in[par][:, :, :], x_g[group]).then_inc(x_loaded[par], 16)
                sp.dma_start(ctx_in[par][:, :, :], ctx_t[group]).then_inc(ctx_loaded[par], 16)
                sp.dma_start(mask_in[par][:, :], mask_g[group].to_broadcast((P, T))).then_inc(mask_loaded[par], 16)

            load_group(Step(0, 0, False))
            c0 = 0
            for n, w in (("wq", wq), ("wk", wk), ("wv", wv), ("wo", wo), ("w1", w1), ("w2", w2)):
                sp.dma_start(w_raw[:, c0:c0 + w_cols[n]], w).then_inc(w_loaded, 16)
                c0 += w_cols[n]
            for t, v in ((bq_col, bq), (bk_col, bk), (b1_col, b1)):
                sp.dma_start(t[:, :], v).then_inc(consts_loaded, 16)
            for t, v in ((bv_row, bv), (bo_row, bo), (b2_row, b2)):
                sp.dma_start(t[:, 0, :], v.to_broadcast((P, E))).then_inc(consts_loaded, 16)

            def run_step(st):
                if st.has("N") and (st.in_loop or st.k > 0):
                    load_group(st)
                if st.has("C"):
                    if st.in_loop or st.k > LAG["C"]:
                        alone(sp, sp_passed, x2_done, st.count("C", 1, 0))
                    sp.dma_start(x_res[:, :, :], x_g[st.group("C")]).then_inc(res_loaded, 16)
                if st.has("A"):
                    par = st.parity("A")
                    if st.in_loop or st.k > LAG["A"] + 1:
                        alone(sp, sp_passed, shifted_mm, st.count("B", 2 * GB, 0))
                    alone(sp, sp_passed, mask_parts_done, st.count("A", 1, 1))
                    for r in range(3):
                        sp.dma_start(k_rows[par][ROWS_PRODUCTS + r:ROWS_PRODUCTS + r + 1, :, :],
                                     mask_parts[0:1, r:r + 1, :].to_broadcast((1, HEADS, T))).then_inc(k_rows_in[par], 16)

                def max_rows_to_queries(j):
                    par = st.parity("B")
                    alone(sp, sp_passed, max_rows_done, st.count("B", GB, j + 1))
                    sp.dma_start(q_rows[par][ROWS_MASK:ROWS_MAX, :, j * S:(j + 1) * S],
                                 max_rows[:, :]).then_inc(max_rows_in, 16)

                if st.has("B"):
                    max_rows_to_queries(0)
                if st.has("A"):
                    par = st.parity("A")
                    alone(sp, sp_passed, q_split, st.count("A", 3, 3))
                    for n, (qp, _) in enumerate(PAIRS):
                        sp.dma_start(q_rows[par][n * D:(n + 1) * D, :, :].rearrange("d h t -> d (h t)"),
                                     q_parts[:, qp, :, :].rearrange("p a t -> p (a t)")).then_inc(q_rows_in[par], 16)
                if st.has("B"):
                    max_rows_to_queries(1)
                if st.has("F"):
                    alone(sp, sp_passed, y_done, st.count("F", 1, 1))
                    sp.dma_start(out_g[st.group("F")], x2_bias[:, :, :]).then_inc(out_stored, 16)
                if st.has("A"):
                    alone(sp, sp_passed, k_split, st.count("A", 3, 3))
                    for n, (_, kp) in enumerate(PAIRS):
                        sp.dma_start(k_rows[par][n * D:(n + 1) * D, :, :].rearrange("d h t -> d (h t)"),
                                     k_parts[:, kp, :, :].rearrange("p a t -> p (a t)")).then_inc(k_rows_in[par], 16)
                if st.has("B"):
                    alone(sp, sp_passed, attn_out, st.count("B", GB, GB))
                    if st.has("C"):
                        alone(sp, sp_passed, attn_split, st.count("C", 2, 2))
                    for r in range(4):
                        for half, dst in ((0, numer), (1, denom)):
                            p0 = 32 * r + D * half
                            sp.dma_start(dst[64 * (r % 2):64 * (r % 2) + 64, r // 2, :],
                                         attn_raw[p0:p0 + D, :, :]).then_inc(packed, 16)

            over_steps(sp, run_step)
            sp.wait_ge(out_stored, 16 * GROUPS)

        @block.gpsimd
        def _(pool):
            for t in (ident, ident_bf):
                nc.gpsimd.memset(t[:, :], 0.0).then_inc(ident_zeroed, 1)
            pool.wait_ge(ident_zeroed, 2)
            for t in (ident, ident_bf):
                nc.gpsimd.affine_select(out=t[:, :], in_=t[:, :], compare_op=ALU.not_equal, fill=1.0, base=0,
                                        pattern=[[-1, P]], channel_multiplier=1).then_inc(consts_set, 1)
            pair_of_ones = float(np.array([0x3F803F80], np.uint32).view(np.float32)[0])
            fills = [(minus_half[:, :], -0.5)]
            for i in range(2):
                fills += [(q_rows[i][96:128, :, :].bitcast(fp32), pair_of_ones),
                          (k_rows[i][96:128, :, :].bitcast(fp32), pair_of_ones), (v_ones[i][:, :, :, :], 1.0)]
            for done, (dst, value) in enumerate(fills):
                pool.wait_ge(consts_set, 2 + done)
                nc.gpsimd.memset(dst, value).then_inc(consts_set, 1)
            pool.wait_ge(consts_set, 9)

            def run_step(st):
                if st.has("C"):
                    alone(pool, pool_passed, res_loaded, st.count("C", 16, 16))
                    if st.k == LAG["C"]:
                        pool.wait_ge(consts_loaded, 6 * 16)
                    nc.gpsimd.tensor_tensor(x_res[:, :, :], x_res[:, :, :], bo_row[:, :, :].to_broadcast((P, GB, E)),
                                            ALU.add).then_inc(res_bias, 1)
                if st.has("A"):
                    par = st.parity("A")
                    alone(pool, pool_passed, ctx_loaded[par], st.count_alternate("A", 16, 16))
                    alone(pool, pool_passed, v_mm, st.count("A", 1, 0))
                    nc.gpsimd.tensor_scalar(ctx_hi[:, :, :], ctx_in[par][:, :, :], 1.0, 1.0, ALU.mult,
                                            ALU.mult).then_inc(ctx_hi_done, 1)
                    alone(pool, pool_passed, ctx_hi_done, st.count("A", 1, 1))
                    nc.gpsimd.tensor_tensor(ctx_lo[:, :, :], ctx_in[par][:, :, :], ctx_hi[:, :, :].bitcast(fp32),
                                            ALU.subtract).then_inc(ctx_lo_done, 1)
                if st.has("C"):
                    alone(pool, pool_passed, recip_done, st.count("C", 1, 1))
                    nc.gpsimd.tensor_tensor(numer[:, :, :], numer[:, :, :], denom[:, :, :], ALU.mult).then_inc(attn_norm, 1)
                    alone(pool, pool_passed, attn_norm, st.count("C", 1, 1))
                    alone(pool, pool_passed, o_mm, st.count("C", 1, 0))
                    nc.gpsimd.tensor_scalar(attn_hi[:, :, :], numer[:, :, :], 1.0, 1.0, ALU.mult,
                                            ALU.mult).then_inc(attn_split, 1)
                    alone(pool, pool_passed, attn_split, st.count("C", 2, 1))
                    nc.gpsimd.tensor_tensor(attn_lo[:, :, :], numer[:, :, :], attn_hi[:, :, :].bitcast(fp32),
                                            ALU.subtract).then_inc(attn_split, 1)
                if st.has("A"):
                    for hi_done, done, parts, rest, rows_in in ((q_hi_done, q_split, q_parts, q_rest, q_rows_in),
                                                                (k_hi_done, k_split, k_parts, k_rest, k_rows_in)):
                        alone(pool, pool_passed, hi_done, st.count("A", 1, 1))
                        nc.gpsimd.tensor_tensor(rest[:, :, :], rest[:, :, :], parts[:, 0, :, :],
                                                ALU.subtract).then_inc(done, 1)
                        alone(pool, pool_passed, done, st.count("A", 3, 1))
                        nc.gpsimd.tensor_scalar(parts[:, 1, :, :], rest[:, :, :], 1.0, 1.0, ALU.mult,
                                                ALU.mult).then_inc(done, 1)
                        alone(pool, pool_passed, done, st.count("A", 3, 2))
                        nc.gpsimd.tensor_tensor(parts[:, 2, :, :], rest[:, :, :], parts[:, 1, :, :],
                                                ALU.subtract).then_inc(done, 1)
                if st.has("C"):
                    alone(pool, pool_passed, c_var_done, st.count("C", 1, 1))
                    nc.gpsimd.tensor_tensor(c_rstd[:, :], c_var[:, :], minus_half[:, :], ALU.pow).then_inc(c_pow, 1)
                    if st.in_loop or st.k > LAG["C"]:
                        alone(pool, pool_passed, out_stored, st.count("C", 16, 0))
                    nc.gpsimd.tensor_tensor(x2_bias[:, :, :], x2[:, :, :], b2_row[:, :, :].to_broadcast((P, GB, E)),
                                            ALU.add).then_inc(x2_bias_done, 1)

                if st.has("N"):
                    alone(pool, pool_passed, n_var_done, st.count("N", 1, 1))
                    nc.gpsimd.tensor_tensor(n_rstd[:, :], n_var[:, :], minus_half[:, :], ALU.pow).then_inc(n_pow, 1)

            over_steps(pool, run_step)

        @block.scalar
        def _(act):
            def run_step(st):
                def transposed_hi(stage, mm, bank_name, hi, done, used, used_count):
                    alone(act, act_passed, mm, st.count(stage, 1, 1))
                    alone(act, act_passed, used, used_count)
                    nc.scalar.activation(hi[:, :, :], bank[bank_name][:, :, :], ACT.Copy).then_inc(done, 1)

                def exps(j):
                    for half in range(2):
                        alone(act, act_passed, shifted_mm, st.count("B", 2 * GB, 2 * j + half + 1))
                        alone(act, act_passed, attn_mm, st.count("B", GB, j))
                        nc.scalar.activation(probs[:, half * 8:half * 8 + 8, :], scores[half][:, :, :], ACT.Exp,
                                             scale=SCORE_SCALE).then_inc(probs_done, 1)

                def attn_evac(j):
                    alone(act, act_passed, attn_mm, st.count("B", GB, j + 1))
                    if j == 0:
                        alone(act, act_passed, packed, st.count("B", 128, 0))
                    nc.scalar.activation(attn_raw[:, :, j * S:(j + 1) * S], attn_ps[:, :, :], ACT.Copy).then_inc(attn_out, 1)

                def hidden(i):
                    alone(act, act_passed, hid_mm, st.count("C", 4, i + 1))
                    alone(act, act_passed, hid_lo_done, st.count("C", 4, i - 1))
                    for u in range(2):
                        f = 2 * i + u
                        ins = nc.scalar.activation(hid[i % 2][:, u, :], bank["BCAB"[i]][:, u, :], ACT.Relu,
                                                   bias=b1_col[:, f:f + 1])
                    ins.then_inc(hid_out, 1)
                    alone(act, act_passed, hid_out, st.count("C", 4, i + 1))
                    alone(act, act_passed, f_mm, st.count("C", 1, 0))
                    nc.scalar.activation(hid_hi[:, 2 * i:2 * i + 2, :], hid[i % 2][:, :, :], ACT.Copy).then_inc(hid_hi_done, 1)

                if st.has("A"):
                    transposed_hi("A", xnT_mm, "C", xnT_hi, xnT_hi_done, q_mm, st.count("A", 1, 0))
                    if st.k == LAG["A"]:
                        act.wait_ge(consts_loaded, 6 * 16)
                    alone(act, act_passed, q_mm, st.count("A", 1, 1))
                    alone(act, act_passed, q_split, st.count("A", 3, 0))
                    for t in range(KT):
                        ins = nc.scalar.activation(q_rest[:, t, :], bank["B"][:, t, :], ACT.Identity, bias=bq_col[:, t:t + 1])
                    ins.then_inc(q_out, 1)
                    alone(act, act_passed, q_out, st.count("A", 1, 1))
                    if st.in_loop or st.k > LAG["A"]:
                        last = st.before()
                        alone(act, act_passed, q_rows_in[last.parity("A")], last.count_alternate("A", 96, 96))
                    nc.scalar.activation(q_parts[:, 0, :, :], q_rest[:, :, :], ACT.Copy).then_inc(q_hi_done, 1)
                    alone(act, act_passed, k_out, st.count("A", 1, 1))
                    if st.in_loop or st.k > LAG["A"]:
                        last = st.before()
                        alone(act, act_passed, k_rows_in[last.parity("A")], last.count_alternate("A", 144, 144))
                    nc.scalar.activation(k_parts[:, 0, :, :], k_rest[:, :, :], ACT.Copy).then_inc(k_hi_done, 1)
                if st.has("B"):
                    exps(0)
                    attn_evac(0)
                if st.has("C"):
                    transposed_hi("C", x2T_mm, "A", x2T_hi, x2T_hi_done, hid_mm, st.count("C", 4, 0))
                    hidden(0)
                if st.has("B"):
                    exps(1)
                if st.has("C"):
                    hidden(1)
                if st.has("B"):
                    attn_evac(1)
                if st.has("C"):
                    hidden(2)
                    hidden(3)

            over_steps(act, run_step)

        @block.vector
        def _(dve):
            def split_weights(names, n_done):
                for n in names:
                    c0 = sum(list(w_cols.values())[:list(w_cols).index(n)])
                    raw = w_raw[:, c0:c0 + w_cols[n]]
                    dve.wait_ge(w_loaded, 6 * 16)
                    nc.vector.tensor_copy(w_hi[n][:, :], raw).then_inc(w_split_hi, 1)
                    n_done += 1
                    dve.wait_ge(w_split_hi, n_done)
                    nc.vector.tensor_tensor(w_lo[n][:, :], raw, w_hi[n][:, :].bitcast(fp32), ALU.subtract).then_inc(w_split, 1)

            def run_step(st):
                def statistics(stage, src, stats, mv, var, bn, ag, var_done):
                    for j in range(GB):
                        nc.vector.bn_stats(stats[:, j, :], src[:, j, :]).then_inc(bn, 1)
                    for j in range(GB):
                        alone(dve, dve_passed, bn, st.count(stage, GB, GB))
                        nc.vector.bn_aggr(mv[:, j, :], stats[:, j, :]).then_inc(ag, 1)
                    dve.wait_ge(ag, st.count(stage, GB, GB))
                    nc.vector.tensor_scalar_add(var[:, :], mv[:, :, 1], EPS).then_inc(var_done, 1)

                def normalise(stage, src, mv, rstd, pow_done, dst, done):
                    alone(dve, dve_passed, pow_done, st.count(stage, 1, 1))
                    for j in range(GB):
                        nc.vector.tensor_scalar(dst[:, j, :], src[:, j, :], mv[:, j, 0:1], rstd[:, j:j + 1],
                                                ALU.subtract, ALU.mult).then_inc(done, 1)

                def maxima(j):
                    for half in range(2):
                        alone(dve, dve_passed, scores_mm, st.count("B", 2 * GB, 2 * j + half + 1))
                        nc.vector.tensor_reduce(minus_max[:, half * 8:half * 8 + 8], scores[half][:, :, :], axis=AX.X,
                                                op=ALU.max, negate=True).then_inc(max_done, 1)
                    alone(dve, dve_passed, max_done, st.count("B", 2 * GB, 2 * j + 2))
                    alone(dve, dve_passed, maxT_mm, st.count("B", GB, j))
                    nc.vector.tensor_copy(max_parts[:, 0, :], minus_max[:, :]).then_inc(max_split, 1)
                    dve.wait_ge(max_split, st.count("B", 4 * GB, 4 * j + 1))
                    nc.vector.tensor_tensor(max_rest[:, :], minus_max[:, :], max_parts[:, 0, :], ALU.subtract).then_inc(max_split, 1)
                    dve.wait_ge(max_split, st.count("B", 4 * GB, 4 * j + 2))
                    nc.vector.tensor_copy(max_parts[:, 1, :], max_rest[:, :]).then_inc(max_split, 1)
                    dve.wait_ge(max_split, st.count("B", 4 * GB, 4 * j + 3))
                    nc.vector.tensor_tensor(max_parts[:, 2, :], max_rest[:, :], max_parts[:, 1, :], ALU.subtract).then_inc(max_split, 1)
                    dve.wait_ge(maxT_mm, st.count("B", GB, j + 1))
                    alone(dve, dve_passed, max_rows_in, st.count("B", 16 * GB, 16 * j))
                    nc.vector.tensor_copy(max_rows[:, :], max_ps).then_inc(max_rows_done, 1)

                def transposed_lo(stage, bank_name, hi, lo, hi_done, done):
                    alone(dve, dve_passed, hi_done, st.count(stage, 1, 1))
                    nc.vector.tensor_tensor(lo[:, :, :], bank[bank_name][:, :, :], hi[:, :, :].bitcast(fp32),
                                            ALU.subtract).then_inc(done, 1)

                def hidden_lo(i):
                    alone(dve, dve_passed, hid_hi_done, st.count("C", 4, i + 1))
                    nc.vector.tensor_tensor(hid_lo[:, 2 * i:2 * i + 2, :], hid[i % 2][:, :, :],
                                            hid_hi[:, 2 * i:2 * i + 2, :].bitcast(fp32), ALU.subtract).then_inc(hid_lo_done, 1)

                if st.has("A"):
                    transposed_lo("A", "C", xnT_hi, xnT_lo, xnT_hi_done, xnT_lo_done)
                    par = st.parity("A")
                    alone(dve, dve_passed, mask_loaded[par], st.count_alternate("A", 16, 16))
                    nc.vector.tensor_scalar(keep[:, :], mask_in[par][:, :], 0.0, None, ALU.not_equal).then_inc(keep_done, 1)
                    if st.in_loop or st.k > LAG["A"]:
                        last = st.before()
                        alone(dve, dve_passed, k_rows_in[last.parity("A")], last.count_alternate("A", 144, 144))
                    for r, part in enumerate(split3(MASKED)):
                        ins = nc.vector.tensor_scalar(mask_parts[:, r, :], mask_in[par][0:1, :], 0.0, part,
                                                      ALU.is_equal, ALU.mult)
                    ins.then_inc(mask_parts_done, 1)
                if st.has("B"):
                    maxima(0)
                if st.has("A"):
                    alone(dve, dve_passed, k_mm, st.count("A", 1, 1))
                    alone(dve, dve_passed, keep_done, st.count("A", 1, 1))
                    alone(dve, dve_passed, k_split, st.count("A", 3, 0))
                    if st.k == LAG["A"]:
                        dve.wait_ge(consts_loaded, 6 * 16)
                    for t in range(KT):
                        ins = nc.vector.scalar_tensor_tensor(out=k_rest[:, t, :], in0=bank["C"][:, t, :],
                                                             scalar=bk_col[:, t:t + 1], in1=keep[:, :],
                                                             op0=ALU.add, op1=ALU.mult)
                    ins.then_inc(k_out, 1)
                if st.has("C"):
                    alone(dve, dve_passed, packed, st.count("C", 128, 128))
                    nc.vector.reciprocal(denom[:, :, :], denom[:, :, :]).then_inc(recip_done, 1)
                if st.has("A"):
                    alone(dve, dve_passed, v_mm, st.count("A", 1, 1))
                    for j in range(GB):
                        ins = nc.vector.tensor_tensor(
                            v_ones[par][:, j, :, 0:D], bank["C"][:, j, :].rearrange("p (h d) -> p h d", d=D),
                            bv_row[:, 0, :].rearrange("p (h d) -> p h d", d=D), ALU.add)
                    ins.then_inc(v_done, 1)
                if st.has("C"):
                    alone(dve, dve_passed, o_mm, st.count("C", 1, 1))
                    alone(dve, dve_passed, res_bias, st.count("C", 1, 1))
                    alone(dve, dve_passed, x2_bias_done, st.count("C", 1, 0))
                    nc.vector.tensor_tensor(x2[:, :, :], bank["B"][:, :, :], x_res[:, :, :], ALU.add).then_inc(x2_done, 1)
                    alone(dve, dve_passed, x2_done, st.count("C", 1, 1))
                    statistics("C", x2, c_stats, c_mv, c_var, c_bn, c_ag, c_var_done)
                if st.has("B"):
                    maxima(1)
                if st.has("C"):
                    alone(dve, dve_passed, x2T_mm, st.count("C", 1, 0))
                    normalise("C", x2, c_mv, c_rstd, c_pow, x2n, x2n_done)
                if st.has("F"):
                    alone(dve, dve_passed, f_mm, st.count("F", 1, 1))
                    alone(dve, dve_passed, x2_bias_done, st.count("F", 1, 1))
                    nc.vector.tensor_tensor(x2_bias[:, :, :], bank["A"][:, :, :], x2_bias[:, :, :], ALU.add).then_inc(y_done, 1)
                if st.has("C"):
                    transposed_lo("C", "A", x2T_hi, x2T_lo, x2T_hi_done, x2T_lo_done)
                    for i in range(4):
                        hidden_lo(i)
                if st.has("N"):
                    par = st.parity("N")
                    alone(dve, dve_passed, x_loaded[par], st.count_alternate("N", 16, 16))
                    statistics("N", x_in[par], n_stats, n_mv, n_var, n_bn, n_ag, n_var_done)
                    alone(dve, dve_passed, xnT_mm, st.count("N", 1, 0))
                    normalise("N", x_in[par], n_mv, n_rstd, n_pow, xn, xn_done)
                if not st.in_loop and st.k == 0:
                    split_weights(("wq", "wk", "wv"), 0)
                if not st.in_loop and st.k == 1:
                    split_weights(("wo", "w1", "w2"), 3)

            over_steps(dve, run_step)

        @block.tensor
        def _(pe):
            w = {n: (w_hi[n][:, :].rearrange("p (k m) -> p k m", k=KT if n != "w2" else FT),
                     w_lo[n][:, :].rearrange("p (k m) -> p k m", k=KT if n != "w2" else FT)) for n in w_cols}

            def three_passes(out_ap, lhs, rhs, steps, first=True, last=True):
                runs = [(a, b, k) for k in steps for a, b in ((1, 0), (0, 1), (0, 0))]
                for n, (a, b, k) in enumerate(runs):
                    ins = nc.tensor.matmul(out_ap, lhs(a, k), rhs(b, k), start=first and n == 0,
                                           stop=last and n == len(runs) - 1)
                return ins

            def run_step(st):
                def score_rows(j, rows, done, slot_free):
                    par = st.parity("B")
                    for half in range(2):
                        slot_free(half)
                        for i in range(8):
                            h = half * 8 + i
                            ks = k_rows[par][0:rows, h, j * S:(j + 1) * S]
                            qs = q_rows[par][0:rows, h, j * S:(j + 1) * S]
                            a, b = (qs, ks) if rows == ROWS_MASK else (ks, qs)
                            ins = nc.tensor.matmul(scores[half][:, i, :], a, b, start=True, stop=True)
                        ins.then_inc(done, 1)

                def plain_scores(j):
                    if j == 0:
                        par = st.parity("B")
                        pe.wait_ge(q_rows_in[par], st.count_alternate("B", 96, 96))
                        pe.wait_ge(k_rows_in[par], st.count_alternate("B", 144, 144))
                        if st.k == LAG["B"]:
                            pe.wait_ge(consts_set, 9)

                    def slot_free(half):
                        if st.in_loop or st.k > LAG["B"] or j > 0:
                            pe.wait_ge(probs_done, st.count("B", 2 * GB, 2 * j - 1 + half))
                    score_rows(j, ROWS_MASK, scores_mm, slot_free)

                def max_transpose(j):
                    alone(pe, pe_passed, max_split, st.count("B", 4 * GB, 4 * j + 4))
                    alone(pe, pe_passed, attn_out, st.count("B", GB, j))
                    nc.tensor.transpose(max_ps, max_parts[:, :, :].rearrange("p a h -> p (a h)"),
                                        ident_bf[:, :]).then_inc(maxT_mm, 1)

                def shifted_scores(j):
                    pe.wait_ge(max_rows_in, st.count("B", 16 * GB, 16 * (j + 1)))

                    def slot_free(half):
                        pe.wait_ge(max_done, st.count("B", 2 * GB, 2 * j + half + 1))
                    score_rows(j, ROWS_MAX, shifted_mm, slot_free)

                def attend(j):
                    par = st.parity("B")
                    pe.wait_ge(probs_done, st.count("B", 2 * GB, 2 * j + 2))
                    pe.wait_ge(v_done, st.count("B", 1, 1))
                    for quad in range(QUADS):
                        for r in range(4):
                            h = 4 * quad + r
                            ins = nc.tensor.matmul(attn_ps[32 * r:32 * r + 32, quad, :], v_ones[par][:, j, h, :],
                                                   probs[:, h, :], start=True, stop=True)
                    ins.then_inc(attn_mm, 1)

                def transposes(stage, name, bank_name, src, src_done, mm):
                    bank_free(pe, st, name)
                    pe.wait_ge(src_done, st.count(stage, GB, GB))
                    for t in range(KT):
                        for j in range(GB):
                            ins = nc.tensor.transpose(bank[bank_name][:, t, j * S:(j + 1) * S],
                                                      src[:, j, t * P:(t + 1) * P], ident[:, :])
                    ins.then_inc(mm, 1)

                def project(name, w_name, hi, lo, mm):
                    bank_free(pe, st, name)
                    for t in range(KT):
                        ins = three_passes(bank["B" if name == "q" else "C"][:, t, :],
                                           lambda a, k: w[w_name][a][:, k, t * P:(t + 1) * P],
                                           lambda b, k: (hi, lo)[b][:, k, :], range(KT))
                    ins.then_inc(mm, 1)

                def rows_out(name, bank_name, pair, w_name, mm):
                    bank_free(pe, st, name)
                    for j in range(GB):
                        ins = three_passes(bank[bank_name][:, j, :],
                                           lambda a, k: pair[a][:, k, j * S:(j + 1) * S],
                                           lambda b, k: w[w_name][b][:, k, :], range(KT))
                    ins.then_inc(mm, 1)

                def second_product(j, half):
                    steps = range(half * FT // 2, (half + 1) * FT // 2)
                    if j == 0 and half == 0:
                        bank_free(pe, st, "f")
                        pe.wait_ge(hid_lo_done, st.count("F", 4, 4))
                    ins = three_passes(bank["A"][:, j, :], lambda a, k: (hid_hi, hid_lo)[a][:, k, j * S:(j + 1) * S],
                                       lambda b, k: w["w2"][b][:, k, :], steps, half == 0, half == 1)
                    if j == GB - 1 and half == 1:
                        ins.then_inc(f_mm, 1)

                def first_product(i):
                    bank_free(pe, st, f"h{i}")
                    for u in range(2):
                        f = 2 * i + u
                        ins = three_passes(bank["BCAB"[i]][:, u, :], lambda a, k: w["w1"][a][:, k, f * P:(f + 1) * P],
                                           lambda b, k: (x2T_hi, x2T_lo)[b][:, k, :], range(KT))
                    ins.then_inc(hid_mm, 1)

                a, b, c, f = st.has("A"), st.has("B"), st.has("C"), st.has("F")
                if b:
                    plain_scores(0)
                if a:
                    if st.k == LAG["A"]:
                        pe.wait_ge(w_split, 3)
                        pe.wait_ge(consts_set, 9)
                    transposes("A", "xnT", "C", xn, xn_done, xnT_mm)
                if f:
                    second_product(0, 0)
                if a:
                    pe.wait_ge(xnT_lo_done, st.count("A", 1, 1))
                    project("q", "wq", xnT_hi, xnT_lo, q_mm)
                if b:
                    max_transpose(0)
                if f:
                    second_product(0, 1)
                if a:
                    pe.wait_ge(ctx_lo_done, st.count("A", 1, 1))
                    project("k", "wk", ctx_hi, ctx_lo, k_mm)
                if b:
                    shifted_scores(0)
                if f:
                    second_product(1, 0)
                if b:
                    attend(0)
                    plain_scores(1)
                if a:
                    rows_out("v", "C", (ctx_hi, ctx_lo), "wv", v_mm)
                if c:
                    if st.k == LAG["C"]:
                        pe.wait_ge(w_split, 6)
                    pe.wait_ge(attn_split, st.count("C", 2, 2))
                    rows_out("o", "B", (attn_hi, attn_lo), "wo", o_mm)
                if b:
                    max_transpose(1)
                if f:
                    second_product(1, 1)
                if c:
                    transposes("C", "x2T", "A", x2n, x2n_done, x2T_mm)
                    pe.wait_ge(x2T_lo_done, st.count("C", 1, 1))
                    first_product(0)
                if b:
                    shifted_scores(1)
                if c:
                    first_product(1)
                    first_product(2)
                if b:
                    attend(1)
                if c:
                    first_product(3)

            over_steps(pe, run_step)


_INS = ["x", "ctx_t", "mask", "wq", "wk", "wv", "wo", "w1", "w2", "bq", "bk", "bv", "bo", "b1", "b2"]


def kernel(**inputs):
    import concourse.bacc as bacc
    from concourse.bass_utils import run_bass_kernel_spmd

    n = {k.replace("L0_xattn_", "").replace("L0_ffn_", ""): np.asarray(v) for k, v in inputs.items()}

    def tiles(w):
        return w.reshape(w.shape[0] // P, P, w.shape[1]).transpose(1, 0, 2).reshape(P, -1)

    def by_dim(w):
        return w.reshape(w.shape[0], HH, KT, D).transpose(0, 2, 3, 1).reshape(w.shape[0], E)

    wo = n["Wo"].reshape(QUADS, KT, 2, D, E).transpose(1, 2, 3, 0, 4).reshape(E, E)
    arrays = {
        "x": n["x"],
        "ctx_t": n["ctx_1024"].reshape(GROUPS, GB, S, KT, P).transpose(0, 4, 3, 1, 2).reshape(GROUPS, P, KT, T),
        "mask": n["mask_Bx1x1xS2_if1"],
        "wq": tiles(by_dim(n["Wq"])), "wk": tiles(by_dim(n["Wk"])), "wv": tiles(n["Wv"]), "wo": tiles(wo),
        "w1": tiles(n["W1"]), "w2": tiles(n["W2"]),
        "bq": by_dim(n["bq"][None]).reshape(KT, P).T, "bk": by_dim(n["bk"][None]).reshape(KT, P).T,
        "bv": n["bv"][None], "bo": n["bo"][None], "b1": n["b1"].reshape(FT, P).T, "b2": n["b2"][None],
    }
    arrays = {k: np.ascontiguousarray(v) for k, v in arrays.items()}
    nc = bacc.Bacc("TRN2", target_bir_lowering=False, num_devices=1)
    args = [nc.dram_tensor(f"in_{k}", arrays[k].shape, mybir.dt.from_np(arrays[k].dtype), kind="ExternalInput").ap()
            for k in _INS]
    out = nc.dram_tensor("out", (B, S, E), mybir.dt.float32, kind="ExternalOutput").ap()
    build(nc, *args, out)
    r = run_bass_kernel_spmd(nc, [{f"in_{k}": arrays[k] for k in _INS}], core_ids=[0])
    return r.results[0]["out"]
```

```python
import numpy as np
import concourse.bass as bass
from concourse import mybir
from contextlib import ExitStack


B, S, E, HEADS, F = 64, 128, 256, 16, 1024
D = E // HEADS
P = 128
GB = 2
T = GB * S
GROUPS = B // GB
KT = E // P
FT = F // P
HH = P // D
QUADS = HEADS // 4
EPS = 1e-5
MASKED = float(np.float32(-1e20))
SCORE_SCALE = 1.0 / float(np.sqrt(D))
PAIRS = ((0, 0), (0, 1), (1, 0), (0, 2), (1, 1), (2, 0))
ROWS_PRODUCTS = len(PAIRS) * D
ROWS_MASK = ROWS_PRODUCTS + 3
ROWS_MAX = ROWS_MASK + 3


def stage_lags():
    return {"N": 0, "A": 1, "B": 2, "C": 3, "G": 4, "F": 5}


LAG = stage_lags()


class Step:

    def __init__(self, pair, k, in_loop):
        self.pair, self.k, self.in_loop = pair, k, in_loop

    def has(self, stage):
        return self.in_loop or 0 <= self.k - LAG[stage] < GROUPS

    def before(self):
        return Step(self.pair, self.k - 1, self.in_loop)

    def parity(self, stage):
        return (self.k - LAG[stage]) % 2

    def group(self, stage):
        return self.pair * 2 + (self.k - LAG[stage])

    def count(self, stage, per, done):
        return self.pair * (2 * per) + (per * (self.k - LAG[stage]) + done)

    def count_alternate(self, stage, per, done):
        return self.pair * per + (per * ((self.k - LAG[stage]) // 2) + done)


def split3(value):
    parts, rest = [], np.float32(value)
    for _ in range(3):
        bits = np.array(rest, np.float32).view(np.uint32).astype(np.uint64)
        bits = ((bits + 0x7FFF + ((bits >> 16) & 1)) & 0xFFFF0000).astype(np.uint32)
        part = bits.view(np.float32)
        parts.append(float(part))
        rest = np.float32(rest - part)
    return parts


def build(nc, x, ctx_t, mask, wq, wk, wv, wo, w1, w2, bq, bk, bv, bo, b1, b2, out):
    fp32, f32r, bf16, i32 = mybir.dt.float32, mybir.dt.float32r, mybir.dt.bfloat16, mybir.dt.int32
    ALU, ACT, AX = mybir.AluOpType, mybir.ActivationFunctionType, mybir.AxisListType

    x_g = x.rearrange("(g j) p e -> g p j e", j=GB)
    out_g = out.rearrange("(g j) p e -> g p j e", j=GB)
    mask_g = mask.rearrange("(g j) a b k -> g (a b) (j k)", j=GB)

    ctx = ExitStack()
    with ctx:
        def sb(name, shape, dt=fp32):
            return ctx.enter_context(nc.sbuf_tensor(name, shape, dt))

        def sem(name):
            return ctx.enter_context(nc.semaphore(name))

        w_cols = {"wq": KT * E, "wk": KT * E, "wv": KT * E, "wo": KT * E, "w1": KT * F, "w2": FT * E}
        w_raw = sb("w_raw", [P, sum(w_cols.values())])
        w_hi = {n: sb(f"{n}_hi", [P, c], f32r) for n, c in w_cols.items()}
        w_lo = {n: sb(f"{n}_lo", [P, c], f32r) for n, c in w_cols.items()}
        bq_col, bk_col, b1_col = sb("bq_col", [P, KT]), sb("bk_col", [P, KT]), sb("b1_col", [P, FT])
        bv_row, bo_row, b2_row = sb("bv_row", [P, 1, E]), sb("bo_row", [P, 1, E]), sb("b2_row", [P, 1, E])
        ident = sb("ident", [P, P])
        ident_bf = sb("ident_bf", [P, P], bf16)
        minus_half = sb("minus_half", [P, GB])

        x_in = [sb(f"x_in{i}", [P, GB, E]) for i in range(2)]
        n_stats, n_mv = sb("n_stats", [P, GB, 6]), sb("n_mv", [P, GB, 2])
        n_var, n_rstd = sb("n_var", [P, GB]), sb("n_rstd", [P, GB])
        xn = sb("xn", [P, GB, E])
        ctx_in = [sb(f"ctx_in{i}", [P, KT, T]) for i in range(2)]
        mask_in = [sb(f"mask_in{i}", [P, T], i32) for i in range(2)]
        keep = sb("keep", [P, T])
        mask_parts, masked_part = sb("mask_parts", [3, T], bf16), sb("masked_part", [3, 1])
        ctx_hi, ctx_lo = sb("ctx_hi", [P, KT, T], f32r), sb("ctx_lo", [P, KT, T], f32r)
        xnT_hi, xnT_lo = sb("xnT_hi", [P, KT, T], f32r), sb("xnT_lo", [P, KT, T], f32r)
        q_rest, k_rest = sb("q_rest", [P, KT, T]), sb("k_rest", [P, KT, T])
        q_parts, k_parts = sb("q_parts", [P, 3, KT, T], bf16), sb("k_parts", [P, 3, KT, T], bf16)
        q_rows = [sb(f"q_rows{i}", [P, HEADS, T], bf16) for i in range(2)]
        k_rows = [sb(f"k_rows{i}", [P, HEADS, T], bf16) for i in range(2)]
        v_ones = [sb(f"v_ones{i}", [P, GB, HEADS, D, 2]) for i in range(2)]
        minus_max, max_rest = sb("minus_max", [P, HEADS]), sb("max_rest", [P, HEADS])
        max_parts = sb("max_parts", [P, 3, HEADS], bf16)
        max_rows = sb("max_rows", [3 * HEADS, S], bf16)
        probs = sb("probs", [P, HEADS, S])
        attn_raw = sb("attn_raw", [P, QUADS, T])
        numer, denom = sb("numer", [P, KT, T]), sb("denom", [P, KT, T])
        attn_hi, attn_lo = sb("attn_hi", [P, KT, T], f32r), sb("attn_lo", [P, KT, T], f32r)
        x_res, x2 = sb("x_res", [P, GB, E]), sb("x2", [P, GB, E])
        x2_bias = [sb(f"x2_bias{i}", [P, GB, E]) for i in range(2)]
        c_stats, c_mv = sb("c_stats", [P, GB, 6]), sb("c_mv", [P, GB, 2])
        c_var, c_rstd = sb("c_var", [P, GB]), sb("c_rstd", [P, GB])
        x2n = sb("x2n", [P, GB, E])
        x2T_hi, x2T_lo = sb("x2T_hi", [P, KT, T], f32r), sb("x2T_lo", [P, KT, T], f32r)
        hid = [sb(f"hid{i}", [P, 2, T]) for i in range(2)]
        hid_hi, hid_lo = sb("hid_hi", [P, FT, T], f32r), sb("hid_lo", [P, FT, T], f32r)

        scores = [ctx.enter_context(nc.psum_tensor(f"scores{i}", [P, HEADS // 2, S], fp32)) for i in range(2)]
        attn_ps = ctx.enter_context(nc.psum_tensor("attn_ps", [P, QUADS, S], fp32))
        bank = {n: ctx.enter_context(nc.psum_tensor(f"bank_{n}", [P, 2, T], fp32)) for n in "ABC"}
        max_ps = attn_ps[:, :, :].rearrange("p a b -> p (a b)").bitcast(bf16)[0:3 * HEADS, 0:S]

        w_loaded, consts_loaded, w_split_hi, w_split = sem("w_loaded"), sem("consts_loaded"), sem("w_split_hi"), sem("w_split")
        ident_zeroed, consts_set, masked_set = sem("ident_zeroed"), sem("consts_set"), sem("masked_set")
        x_loaded, ctx_loaded = [sem("x_loaded0"), sem("x_loaded1")], [sem("ctx_loaded0"), sem("ctx_loaded1")]
        mask_loaded = [sem("mask_loaded0"), sem("mask_loaded1")]
        res_loaded, out_stored = sem("res_loaded"), [sem("out_stored0"), sem("out_stored1")]
        n_bn, n_ag, n_var_done, n_pow = sem("n_bn"), sem("n_ag"), sem("n_var_done"), sem("n_pow")
        xn_done, xnT_mm, xnT_hi_done, xnT_lo_done = sem("xn_done"), sem("xnT_mm"), sem("xnT_hi_done"), sem("xnT_lo_done")
        keep_done, mask_parts_done = sem("keep_done"), sem("mask_parts_done")
        ctx_hi_done, ctx_lo_done = sem("ctx_hi_done"), sem("ctx_lo_done")
        q_mm, k_mm, v_mm = sem("q_mm"), sem("k_mm"), sem("v_mm")
        q_out, k_out, q_hi_done, k_hi_done = sem("q_out"), sem("k_out"), sem("q_hi_done"), sem("k_hi_done")
        q_split, k_split, v_done = sem("q_split"), sem("k_split"), sem("v_done")
        q_rows_in, k_rows_in = [sem("q_rows_in0"), sem("q_rows_in1")], [sem("k_rows_in0"), sem("k_rows_in1")]
        scores_mm, max_done, max_split, maxT_mm, max_rows_done = sem("scores_mm"), sem("max_done"), sem("max_split"), sem("maxT_mm"), sem("max_rows_done")
        max_rows_in, shifted_mm, probs_done, attn_mm, attn_out = sem("max_rows_in"), sem("shifted_mm"), sem("probs_done"), sem("attn_mm"), sem("attn_out")
        packed = sem("packed")
        recip_done, attn_norm, attn_split, o_mm = sem("recip_done"), sem("attn_norm"), sem("attn_split"), sem("o_mm")
        res_bias, x2_done, x2_bias_done = sem("res_bias"), sem("x2_done"), sem("x2_bias_done")
        c_bn, c_ag, c_var_done, c_pow = sem("c_bn"), sem("c_ag"), sem("c_var_done"), sem("c_pow")
        x2n_done, x2T_mm, x2T_hi_done, x2T_lo_done = sem("x2n_done"), sem("x2T_mm"), sem("x2T_hi_done"), sem("x2T_lo_done")
        hid_mm, hid_out, hid_hi_done, hid_lo_done = sem("hid_mm"), sem("hid_out"), sem("hid_hi_done"), sem("hid_lo_done")
        f_mm, y_done = sem("f_mm"), sem("y_done")
        act_passed, sp_passed, pool_passed, dve_passed, pe_passed = sem("act_passed"), sem("sp_passed"), sem("pool_passed"), sem("dve_passed"), sem("pe_passed")

        def alone(eng, passed, semaphore, value):
            if isinstance(value, int):
                if value > 0:
                    eng.wait_ge(semaphore, value)
            else:
                eng.wait_ge(semaphore, value)
                eng.sem_inc(passed, 1)

        FILLS = [("x2T", "G", "B", x2T_lo_done, 1), ("xnT", "A", "C", xnT_lo_done, 1), ("q", "A", "B", q_out, 1),
                 ("k", "A", "C", k_out, 1), ("h0", "G", "A", hid_out, 4), ("h1", "G", "B", hid_out, 4),
                 ("h2", "G", "C", hid_out, 4), ("h3", "G", "A", hid_out, 4), ("v", "A", "B", v_done, 1),
                 ("o", "C", "C", x2_done, 1), ("f", "G", "A", y_done, 1)]
        BANK_OF = {name: bank[b] for name, _, b, _, _ in FILLS}

        def bank_free(eng, st, name):
            names = [f[0] for f in FILLS]
            me = FILLS[names.index(name)]
            here = [(st, f) for f in FILLS[:names.index(name)] if f[2] == me[2] and st.has(f[1])]
            prev, back = st, []
            while not here and not back:
                prev = prev.before()
                if not prev.in_loop and prev.k < 0:
                    return
                back = [(prev, f) for f in FILLS if f[2] == me[2] and prev.has(f[1])]
            at, f = (here or back)[-1]
            done = 1 if f[4] == 1 else int(f[0][1:]) + 1
            eng.wait_ge(f[3], at.count(f[1], f[4], done))

        def over_steps(eng, run_step):
            first = LAG["F"] + (GROUPS - LAG["F"]) % 2
            for k in range(first):
                run_step(Step(0, k, False))
            with eng.Fori(0, (GROUPS - first) // 2) as pair:
                run_step(Step(pair, first, True))
                run_step(Step(pair, first + 1, True))
            for k in range(GROUPS, GROUPS + LAG["F"]):
                run_step(Step(0, k, False))

        block = ctx.enter_context(nc.Block())

        @block.sync
        def _(sp):
            def load_group(st):
                group, par = st.group("N"), st.parity("N")
                if st.in_loop or st.k > 1:
                    alone(sp, sp_passed, xn_done, st.count("A", GB, 0))
                    alone(sp, sp_passed, ctx_lo_done, st.count("A", 1, 0))
                    alone(sp, sp_passed, keep_done, st.count("A", 1, 0))
                    alone(sp, sp_passed, mask_parts_done, st.count("A", 1, 0))
                sp.dma_start(x_in[par][:, :, :], x_g[group]).then_inc(x_loaded[par], 16)
                sp.dma_start(ctx_in[par][:, :, :], ctx_t[group]).then_inc(ctx_loaded[par], 16)
                sp.dma_start(mask_in[par][:, :], mask_g[group].to_broadcast((P, T))).then_inc(mask_loaded[par], 16)

            load_group(Step(0, 0, False))
            c0 = 0
            for n, w in (("wq", wq), ("wk", wk), ("wv", wv), ("wo", wo), ("w1", w1), ("w2", w2)):
                sp.dma_start(w_raw[:, c0:c0 + w_cols[n]], w).then_inc(w_loaded, 16)
                c0 += w_cols[n]
            for t, v in ((bq_col, bq), (bk_col, bk), (b1_col, b1)):
                sp.dma_start(t[:, :], v).then_inc(consts_loaded, 16)
            for t, v in ((bv_row, bv), (bo_row, bo), (b2_row, b2)):
                sp.dma_start(t[:, 0, :], v.to_broadcast((P, E))).then_inc(consts_loaded, 16)

            def run_step(st):
                if st.has("N") and (st.in_loop or st.k > 0):
                    load_group(st)
                if st.has("C"):
                    alone(sp, sp_passed, x2_done, st.count("C", 1, 0))
                    sp.dma_start(x_res[:, :, :], x_g[st.group("C")]).then_inc(res_loaded, 16)
                if st.has("F"):
                    alone(sp, sp_passed, y_done, st.count("F", 1, 1))
                    sp.dma_start(out_g[st.group("F")], x2_bias[st.parity("F")][:, :, :]).then_inc(out_stored[st.parity("F")], 16)
                if st.has("A"):
                    par = st.parity("A")
                    if st.in_loop or st.k > LAG["A"] + 1:
                        alone(sp, sp_passed, shifted_mm, st.count("B", 2 * GB, 0))
                    alone(sp, sp_passed, mask_parts_done, st.count("A", 1, 1))
                    sp.dma_start(k_rows[par][ROWS_PRODUCTS:ROWS_MASK, :, :],
                                 mask_parts[:, :].unsqueeze(1).to_broadcast((3, HEADS, T))).then_inc(k_rows_in[par], 16)
                    alone(sp, sp_passed, q_split, st.count("A", 3, 3))
                    for n, (qp, _) in enumerate(PAIRS):
                        sp.dma_start(q_rows[par][n * D:(n + 1) * D, :, :].rearrange("d h t -> d (h t)"),
                                     q_parts[:, qp, :, :].rearrange("p a t -> p (a t)")).then_inc(q_rows_in[par], 16)
                    alone(sp, sp_passed, k_split, st.count("A", 3, 3))
                    for n, (_, kp) in enumerate(PAIRS):
                        sp.dma_start(k_rows[par][n * D:(n + 1) * D, :, :].rearrange("d h t -> d (h t)"),
                                     k_parts[:, kp, :, :].rearrange("p a t -> p (a t)")).then_inc(k_rows_in[par], 16)
                if st.has("B"):
                    alone(sp, sp_passed, attn_out, st.count("B", GB, GB))
                    if st.has("C"):
                        alone(sp, sp_passed, attn_split, st.count("C", 2, 2))
                    for half, dst in ((0, numer), (1, denom)):
                        sp.dma_start(dst[:, :, :], attn_raw[half::2, :, :]).then_inc(packed, 16)

            over_steps(sp, run_step)
            for stored in out_stored:
                sp.wait_ge(stored, 16 * GROUPS // 2)

        @block.gpsimd
        def _(pool):
            for t in (ident, ident_bf):
                nc.gpsimd.memset(t[:, :], 0.0).then_inc(ident_zeroed, 1)
            pool.wait_ge(ident_zeroed, 2)
            for t in (ident, ident_bf):
                nc.gpsimd.affine_select(out=t[:, :], in_=t[:, :], compare_op=ALU.not_equal, fill=1.0, base=0,
                                        pattern=[[-1, P]], channel_multiplier=1).then_inc(consts_set, 1)
            pair_of_ones = float(np.array([0x3F803F80], np.uint32).view(np.float32)[0])
            fills = [(minus_half[:, :], -0.5)]
            for i in range(2):
                fills += [(q_rows[i][96:128, :, :].bitcast(fp32), pair_of_ones),
                          (k_rows[i][96:128, :, :].bitcast(fp32), pair_of_ones), (v_ones[i][:, :, :, :, :], 1.0)]
            for done, (dst, value) in enumerate(fills):
                pool.wait_ge(consts_set, 2 + done)
                nc.gpsimd.memset(dst, value).then_inc(consts_set, 1)
            pool.wait_ge(consts_set, 9)

            def split_in_three(st, hi_done, done, parts, rest):
                alone(pool, pool_passed, hi_done, st.count("A", 1, 1))
                nc.gpsimd.tensor_tensor(rest[:, :, :], rest[:, :, :], parts[:, 0, :, :], ALU.subtract).then_inc(done, 1)
                alone(pool, pool_passed, done, st.count("A", 3, 1))
                nc.gpsimd.tensor_scalar(parts[:, 1, :, :], rest[:, :, :], 1.0, 1.0, ALU.mult, ALU.mult).then_inc(done, 1)
                alone(pool, pool_passed, done, st.count("A", 3, 2))
                nc.gpsimd.tensor_tensor(parts[:, 2, :, :], rest[:, :, :], parts[:, 1, :, :], ALU.subtract).then_inc(done, 1)

            def run_step(st):
                if st.has("C"):
                    alone(pool, pool_passed, res_loaded, st.count("C", 16, 16))
                    if st.k == LAG["C"]:
                        pool.wait_ge(consts_loaded, 6 * 16)
                    nc.gpsimd.tensor_tensor(x_res[:, :, :], x_res[:, :, :], bo_row[:, :, :].to_broadcast((P, GB, E)),
                                            ALU.add).then_inc(res_bias, 1)
                if st.has("A"):
                    split_in_three(st, q_hi_done, q_split, q_parts, q_rest)
                    split_in_three(st, k_hi_done, k_split, k_parts, k_rest)
                if st.has("C"):
                    alone(pool, pool_passed, recip_done, st.count("C", 1, 1))
                    nc.gpsimd.tensor_tensor(numer[:, :, :], numer[:, :, :], denom[:, :, :], ALU.mult).then_inc(attn_norm, 1)
                    alone(pool, pool_passed, attn_norm, st.count("C", 1, 1))
                    alone(pool, pool_passed, o_mm, st.count("C", 1, 0))
                    nc.gpsimd.tensor_scalar(attn_hi[:, :, :], numer[:, :, :], 1.0, 1.0, ALU.mult,
                                            ALU.mult).then_inc(attn_split, 1)
                    alone(pool, pool_passed, attn_split, st.count("C", 2, 1))
                    nc.gpsimd.tensor_tensor(attn_lo[:, :, :], numer[:, :, :], attn_hi[:, :, :].bitcast(fp32),
                                            ALU.subtract).then_inc(attn_split, 1)
                if st.has("N"):
                    alone(pool, pool_passed, n_var_done, st.count("N", 1, 1))
                    nc.gpsimd.tensor_tensor(n_rstd[:, :], n_var[:, :], minus_half[:, :], ALU.pow).then_inc(n_pow, 1)
                    par = st.parity("N")
                    alone(pool, pool_passed, ctx_loaded[par], st.count_alternate("N", 16, 16))
                    alone(pool, pool_passed, v_mm, st.count("N", 1, 0))
                    nc.gpsimd.tensor_scalar(ctx_hi[:, :, :], ctx_in[par][:, :, :], 1.0, 1.0, ALU.mult,
                                            ALU.mult).then_inc(ctx_hi_done, 1)
                    alone(pool, pool_passed, ctx_hi_done, st.count("N", 1, 1))
                    nc.gpsimd.tensor_tensor(ctx_lo[:, :, :], ctx_in[par][:, :, :], ctx_hi[:, :, :].bitcast(fp32),
                                            ALU.subtract).then_inc(ctx_lo_done, 1)
                if st.has("C"):
                    alone(pool, pool_passed, c_var_done, st.count("C", 1, 1))
                    nc.gpsimd.tensor_tensor(c_rstd[:, :], c_var[:, :], minus_half[:, :], ALU.pow).then_inc(c_pow, 1)
                    if st.has("F"):
                        alone(pool, pool_passed, out_stored[st.parity("F")], st.count_alternate("F", 16, 16))
                    nc.gpsimd.tensor_tensor(x2_bias[st.parity("C")][:, :, :], x2[:, :, :],
                                            b2_row[:, :, :].to_broadcast((P, GB, E)), ALU.add).then_inc(x2_bias_done, 1)

            over_steps(pool, run_step)

        @block.scalar
        def _(act):
            def run_step(st):
                def transposed_hi(stage, name, mm, hi, done, used, used_count):
                    alone(act, act_passed, mm, st.count(stage, 1, 1))
                    alone(act, act_passed, used, used_count)
                    nc.scalar.activation(hi[:, :, :], BANK_OF[name][:, :, :], ACT.Copy).then_inc(done, 1)

                def max_rows_out(j):
                    alone(act, act_passed, maxT_mm, st.count("B", GB, j + 1))
                    alone(act, act_passed, max_rows_in, st.count("B", 16 * GB, 16 * j))
                    nc.scalar.activation(max_rows[:, :], max_ps, ACT.Copy).then_inc(max_rows_done, 1)
                    alone(act, act_passed, max_rows_done, st.count("B", GB, j + 1))
                    act.dma_start(q_rows[st.parity("B")][ROWS_MASK:ROWS_MAX, :, j * S:(j + 1) * S],
                                  max_rows[:, :]).then_inc(max_rows_in, 16)

                def exps(j, half):
                    alone(act, act_passed, shifted_mm, st.count("B", 2 * GB, 2 * j + half + 1))
                    alone(act, act_passed, attn_mm, st.count("B", GB, j))
                    nc.scalar.activation(probs[:, half * 8:half * 8 + 8, :], scores[half][:, :, :], ACT.Exp,
                                         scale=SCORE_SCALE).then_inc(probs_done, 1)

                def attn_evac(j):
                    alone(act, act_passed, attn_mm, st.count("B", GB, j + 1))
                    if j == 0:
                        alone(act, act_passed, packed, st.count("B", 32, 0))
                    nc.scalar.activation(attn_raw[:, :, j * S:(j + 1) * S], attn_ps[:, :, :], ACT.Copy).then_inc(attn_out, 1)

                def hidden(i):
                    alone(act, act_passed, hid_mm, st.count("G", 4, i + 1))
                    alone(act, act_passed, hid_lo_done, st.count("G", 4, i - 1))
                    for u in range(2):
                        f = 2 * i + u
                        ins = nc.scalar.activation(hid[i % 2][:, u, :], BANK_OF[f"h{i}"][:, u, :], ACT.Relu,
                                                   bias=b1_col[:, f:f + 1])
                    ins.then_inc(hid_out, 1)
                    alone(act, act_passed, hid_out, st.count("G", 4, i + 1))
                    alone(act, act_passed, f_mm, st.count("G", 1, 0))
                    nc.scalar.activation(hid_hi[:, 2 * i:2 * i + 2, :], hid[i % 2][:, :, :], ACT.Copy).then_inc(hid_hi_done, 1)

                def queries_out():
                    if st.k == LAG["A"]:
                        act.wait_ge(consts_loaded, 6 * 16)
                    alone(act, act_passed, q_mm, st.count("A", 1, 1))
                    alone(act, act_passed, q_split, st.count("A", 3, 0))
                    for t in range(KT):
                        ins = nc.scalar.activation(q_rest[:, t, :], BANK_OF["q"][:, t, :], ACT.Identity, bias=bq_col[:, t:t + 1])
                    ins.then_inc(q_out, 1)
                    alone(act, act_passed, q_out, st.count("A", 1, 1))
                    top_part(q_rest, q_parts, q_rows_in, 96, q_hi_done)

                def top_part(rest, parts, rows_in, per, done):
                    if st.in_loop or st.k > LAG["A"]:
                        last = st.before()
                        alone(act, act_passed, rows_in[last.parity("A")], last.count_alternate("A", per, per))
                    nc.scalar.activation(parts[:, 0, :, :], rest[:, :, :], ACT.Copy).then_inc(done, 1)

                if st.has("G"):
                    transposed_hi("G", "x2T", x2T_mm, x2T_hi, x2T_hi_done, hid_mm, st.count("G", 4, 0))
                if st.has("A"):
                    transposed_hi("A", "xnT", xnT_mm, xnT_hi, xnT_hi_done, q_mm, st.count("A", 1, 0))
                if st.has("B"):
                    max_rows_out(0)
                if st.has("A"):
                    queries_out()
                if st.has("B"):
                    exps(0, 0)
                if st.has("A"):
                    alone(act, act_passed, k_out, st.count("A", 1, 1))
                    top_part(k_rest, k_parts, k_rows_in, 112, k_hi_done)
                if st.has("B"):
                    exps(0, 1)
                if st.has("G"):
                    hidden(0)
                    hidden(1)
                if st.has("B"):
                    attn_evac(0)
                if st.has("G"):
                    hidden(2)
                    hidden(3)
                if st.has("B"):
                    max_rows_out(1)
                    exps(1, 0)
                    exps(1, 1)
                    attn_evac(1)

            over_steps(act, run_step)

        @block.vector
        def _(dve):
            for n, r in enumerate((2, 1, 0)):
                if n:
                    dve.wait_ge(masked_set, n)
                nc.vector.memset(masked_part[0:r + 1, :], split3(MASKED)[r]).then_inc(masked_set, 1)
            dve.wait_ge(masked_set, 3)

            def split_weights(names, n_done):
                for n in names:
                    c0 = sum(list(w_cols.values())[:list(w_cols).index(n)])
                    raw = w_raw[:, c0:c0 + w_cols[n]]
                    dve.wait_ge(w_loaded, 6 * 16)
                    nc.vector.tensor_copy(w_hi[n][:, :], raw).then_inc(w_split_hi, 1)
                    n_done += 1
                    dve.wait_ge(w_split_hi, n_done)
                    nc.vector.tensor_tensor(w_lo[n][:, :], raw, w_hi[n][:, :].bitcast(fp32), ALU.subtract).then_inc(w_split, 1)

            def run_step(st):
                def statistics(stage, src, stats, mv, var, bn, ag, var_done):
                    for j in range(GB):
                        nc.vector.bn_stats(stats[:, j, :], src[:, j, :]).then_inc(bn, 1)
                    for j in range(GB):
                        alone(dve, dve_passed, bn, st.count(stage, GB, GB))
                        nc.vector.bn_aggr(mv[:, j, :], stats[:, j, :]).then_inc(ag, 1)
                    dve.wait_ge(ag, st.count(stage, GB, GB))
                    nc.vector.tensor_scalar_add(var[:, :], mv[:, :, 1], EPS).then_inc(var_done, 1)

                def normalise(stage, src, mv, rstd, pow_done, dst, done):
                    alone(dve, dve_passed, pow_done, st.count(stage, 1, 1))
                    for j in range(GB):
                        nc.vector.tensor_scalar(dst[:, j, :], src[:, j, :], mv[:, j, 0:1], rstd[:, j:j + 1],
                                                ALU.subtract, ALU.mult).then_inc(done, 1)

                def maxima(j):
                    for half in range(2):
                        alone(dve, dve_passed, scores_mm, st.count("B", 2 * GB, 2 * j + half + 1))
                        nc.vector.tensor_reduce(minus_max[:, half * 8:half * 8 + 8], scores[half][:, :, :], axis=AX.X,
                                                op=ALU.max, negate=True).then_inc(max_done, 1)
                    alone(dve, dve_passed, max_done, st.count("B", 2 * GB, 2 * j + 2))
                    alone(dve, dve_passed, maxT_mm, st.count("B", GB, j))
                    nc.vector.tensor_copy(max_parts[:, 0, :], minus_max[:, :]).then_inc(max_split, 1)
                    dve.wait_ge(max_split, st.count("B", 4 * GB, 4 * j + 1))
                    nc.vector.tensor_tensor(max_rest[:, :], minus_max[:, :], max_parts[:, 0, :], ALU.subtract).then_inc(max_split, 1)
                    dve.wait_ge(max_split, st.count("B", 4 * GB, 4 * j + 2))
                    nc.vector.tensor_copy(max_parts[:, 1, :], max_rest[:, :]).then_inc(max_split, 1)
                    dve.wait_ge(max_split, st.count("B", 4 * GB, 4 * j + 3))
                    nc.vector.tensor_tensor(max_parts[:, 2, :], max_rest[:, :], max_parts[:, 1, :], ALU.subtract).then_inc(max_split, 1)

                def transposed_lo(stage, name, hi, lo, hi_done, done):
                    alone(dve, dve_passed, hi_done, st.count(stage, 1, 1))
                    nc.vector.tensor_tensor(lo[:, :, :], BANK_OF[name][:, :, :], hi[:, :, :].bitcast(fp32),
                                            ALU.subtract).then_inc(done, 1)

                def hidden_lo(i):
                    alone(dve, dve_passed, hid_hi_done, st.count("G", 4, i + 1))
                    nc.vector.tensor_tensor(hid_lo[:, 2 * i:2 * i + 2, :], hid[i % 2][:, :, :],
                                            hid_hi[:, 2 * i:2 * i + 2, :].bitcast(fp32), ALU.subtract).then_inc(hid_lo_done, 1)

                def mask_out():
                    par = st.parity("A")
                    alone(dve, dve_passed, mask_loaded[par], st.count_alternate("A", 16, 16))
                    nc.vector.tensor_scalar(keep[:, :], mask_in[par][:, :], 0.0, None, ALU.not_equal).then_inc(keep_done, 1)
                    if st.in_loop or st.k > LAG["A"]:
                        last = st.before()
                        alone(dve, dve_passed, k_rows_in[last.parity("A")], last.count_alternate("A", 112, 112))
                    nc.vector.tensor_scalar(mask_parts[:, :], mask_in[par][0:3, :], 0.0, masked_part[:, 0:1],
                                            ALU.is_equal, ALU.mult).then_inc(mask_parts_done, 1)

                def keys_out():
                    alone(dve, dve_passed, k_mm, st.count("A", 1, 1))
                    alone(dve, dve_passed, keep_done, st.count("A", 1, 1))
                    alone(dve, dve_passed, k_split, st.count("A", 3, 0))
                    if st.k == LAG["A"]:
                        dve.wait_ge(consts_loaded, 6 * 16)
                    for t in range(KT):
                        ins = nc.vector.scalar_tensor_tensor(out=k_rest[:, t, :], in0=BANK_OF["k"][:, t, :],
                                                             scalar=bk_col[:, t:t + 1], in1=keep[:, :],
                                                             op0=ALU.add, op1=ALU.mult)
                    ins.then_inc(k_out, 1)

                def values_out():
                    alone(dve, dve_passed, v_mm, st.count("A", 1, 1))
                    for j in range(GB):
                        ins = nc.vector.tensor_tensor(
                            v_ones[st.parity("A")][:, j, :, :, 0], BANK_OF["v"][:, j, :].rearrange("p (h d) -> p h d", d=D),
                            bv_row[:, 0, :].rearrange("p (h d) -> p h d", d=D), ALU.add)
                    ins.then_inc(v_done, 1)

                if st.has("B"):
                    maxima(0)
                if st.has("G"):
                    transposed_lo("G", "x2T", x2T_hi, x2T_lo, x2T_hi_done, x2T_lo_done)
                if st.has("A"):
                    transposed_lo("A", "xnT", xnT_hi, xnT_lo, xnT_hi_done, xnT_lo_done)
                    mask_out()
                if st.has("F"):
                    alone(dve, dve_passed, f_mm, st.count("F", 1, 1))
                    alone(dve, dve_passed, x2_bias_done, st.count("F", 1, 1))
                    y = x2_bias[st.parity("F")]
                    nc.vector.tensor_tensor(y[:, :, :], BANK_OF["f"][:, :, :], y[:, :, :], ALU.add).then_inc(y_done, 1)
                if st.has("N"):
                    par = st.parity("N")
                    alone(dve, dve_passed, x_loaded[par], st.count_alternate("N", 16, 16))
                    statistics("N", x_in[par], n_stats, n_mv, n_var, n_bn, n_ag, n_var_done)
                if st.has("A"):
                    keys_out()
                if st.has("C"):
                    alone(dve, dve_passed, packed, st.count("C", 32, 32))
                    nc.vector.reciprocal(denom[:, :, :], denom[:, :, :]).then_inc(recip_done, 1)
                if st.has("G"):
                    hidden_lo(0)
                    hidden_lo(1)
                if st.has("B"):
                    maxima(1)
                if st.has("G"):
                    hidden_lo(2)
                    hidden_lo(3)
                if st.has("A"):
                    values_out()
                if st.has("C"):
                    alone(dve, dve_passed, o_mm, st.count("C", 1, 1))
                    alone(dve, dve_passed, res_bias, st.count("C", 1, 1))
                    alone(dve, dve_passed, x2_bias_done, st.count("C", 1, 0))
                    nc.vector.tensor_tensor(x2[:, :, :], BANK_OF["o"][:, :, :], x_res[:, :, :], ALU.add).then_inc(x2_done, 1)
                    alone(dve, dve_passed, x2_done, st.count("C", 1, 1))
                    statistics("C", x2, c_stats, c_mv, c_var, c_bn, c_ag, c_var_done)
                if st.has("N"):
                    alone(dve, dve_passed, xnT_mm, st.count("N", 1, 0))
                    normalise("N", x_in[st.parity("N")], n_mv, n_rstd, n_pow, xn, xn_done)
                if st.has("C"):
                    alone(dve, dve_passed, x2T_mm, st.count("C", 1, 0))
                    normalise("C", x2, c_mv, c_rstd, c_pow, x2n, x2n_done)
                if not st.in_loop and st.k == 0:
                    split_weights(("wq", "wk", "wv"), 0)
                if not st.in_loop and st.k == 1:
                    split_weights(("wo", "w1", "w2"), 3)

            over_steps(dve, run_step)

        @block.tensor
        def _(pe):
            w = {n: (w_hi[n][:, :].rearrange("p (k m) -> p k m", k=KT if n != "w2" else FT),
                     w_lo[n][:, :].rearrange("p (k m) -> p k m", k=KT if n != "w2" else FT)) for n in w_cols}

            def three_passes(out_ap, lhs, rhs, steps, first=True, last=True):
                runs = [(a, b, k) for k in steps for a, b in ((1, 0), (0, 1), (0, 0))]
                for n, (a, b, k) in enumerate(runs):
                    ins = nc.tensor.matmul(out_ap, lhs(a, k), rhs(b, k), start=first and n == 0,
                                           stop=last and n == len(runs) - 1)
                return ins

            def run_step(st):
                def score_rows(j, rows, done, slot_free):
                    par = st.parity("B")
                    for half in range(2):
                        slot_free(half)
                        for i in range(8):
                            h = half * 8 + i
                            ks = k_rows[par][0:rows, h, j * S:(j + 1) * S]
                            qs = q_rows[par][0:rows, h, j * S:(j + 1) * S]
                            a, b = (qs, ks) if rows == ROWS_MASK else (ks, qs)
                            ins = nc.tensor.matmul(scores[half][:, i, :], a, b, start=True, stop=True)
                        ins.then_inc(done, 1)

                def plain_scores(j):
                    if j == 0:
                        par = st.parity("B")
                        pe.wait_ge(q_rows_in[par], st.count_alternate("B", 96, 96))
                        pe.wait_ge(k_rows_in[par], st.count_alternate("B", 112, 112))
                        if st.k == LAG["B"]:
                            pe.wait_ge(consts_set, 9)

                    def slot_free(half):
                        if st.in_loop or st.k > LAG["B"] or j > 0:
                            pe.wait_ge(probs_done, st.count("B", 2 * GB, 2 * j - 1 + half))
                    score_rows(j, ROWS_MASK, scores_mm, slot_free)

                def max_transpose(j):
                    alone(pe, pe_passed, max_split, st.count("B", 4 * GB, 4 * j + 4))
                    alone(pe, pe_passed, attn_out, st.count("B", GB, j))
                    nc.tensor.transpose(max_ps, max_parts[:, :, :].rearrange("p a h -> p (a h)"),
                                        ident_bf[:, :]).then_inc(maxT_mm, 1)

                def shifted_scores(j):
                    pe.wait_ge(max_rows_in, st.count("B", 16 * GB, 16 * (j + 1)))

                    def slot_free(half):
                        pe.wait_ge(max_done, st.count("B", 2 * GB, 2 * j + half + 1))
                    score_rows(j, ROWS_MAX, shifted_mm, slot_free)

                def attend(j):
                    par = st.parity("B")
                    pe.wait_ge(probs_done, st.count("B", 2 * GB, 2 * j + 2))
                    pe.wait_ge(v_done, st.count("B", 1, 1))
                    for quad in range(QUADS):
                        for r in range(4):
                            h = 4 * quad + r
                            ins = nc.tensor.matmul(attn_ps[32 * r:32 * r + 32, quad, :],
                                                   v_ones[par][:, j, h, :, :].rearrange("p d a -> p (d a)"),
                                                   probs[:, h, :], start=True, stop=True)
                    ins.then_inc(attn_mm, 1)

                def transposes(stage, name, src, src_done, mm):
                    bank_free(pe, st, name)
                    pe.wait_ge(src_done, st.count(stage, GB, GB))
                    for t in range(KT):
                        for j in range(GB):
                            ins = nc.tensor.transpose(BANK_OF[name][:, t, j * S:(j + 1) * S],
                                                      src[:, j, t * P:(t + 1) * P], ident[:, :])
                    ins.then_inc(mm, 1)

                def project(name, w_name, hi, lo, mm):
                    bank_free(pe, st, name)
                    for t in range(KT):
                        ins = three_passes(BANK_OF[name][:, t, :],
                                           lambda a, k: w[w_name][a][:, k, t * P:(t + 1) * P],
                                           lambda b, k: (hi, lo)[b][:, k, :], range(KT))
                    ins.then_inc(mm, 1)

                def rows_out(name, pair, w_name, mm):
                    bank_free(pe, st, name)
                    for j in range(GB):
                        ins = three_passes(BANK_OF[name][:, j, :],
                                           lambda a, k: pair[a][:, k, j * S:(j + 1) * S],
                                           lambda b, k: w[w_name][b][:, k, :], range(KT))
                    ins.then_inc(mm, 1)

                def second_product(stage, j, half):
                    steps = range(half * FT // 2, (half + 1) * FT // 2)
                    if j == 0:
                        if half == 0:
                            bank_free(pe, st, "f")
                        pe.wait_ge(hid_lo_done, st.count(stage, 4, 2 * half + 2))
                    ins = three_passes(BANK_OF["f"][:, j, :], lambda a, k: (hid_hi, hid_lo)[a][:, k, j * S:(j + 1) * S],
                                       lambda b, k: w["w2"][b][:, k, :], steps, half == 0, half == 1)
                    if j == GB - 1 and half == 1:
                        ins.then_inc(f_mm, 1)

                def first_product(i):
                    bank_free(pe, st, f"h{i}")
                    if i == 0:
                        pe.wait_ge(x2T_lo_done, st.count("G", 1, 1))
                    for u in range(2):
                        f = 2 * i + u
                        ins = three_passes(BANK_OF[f"h{i}"][:, u, :], lambda a, k: w["w1"][a][:, k, f * P:(f + 1) * P],
                                           lambda b, k: (x2T_hi, x2T_lo)[b][:, k, :], range(KT))
                    ins.then_inc(hid_mm, 1)

                a, b, c, g, f = st.has("A"), st.has("B"), st.has("C"), st.has("G"), st.has("F")
                if b:
                    plain_scores(0)
                if f:
                    second_product("F", 1, 0)
                if g:
                    transposes("G", "x2T", x2n, x2n_done, x2T_mm)
                if a:
                    if st.k == LAG["A"]:
                        pe.wait_ge(w_split, 3)
                        pe.wait_ge(consts_set, 9)
                    transposes("A", "xnT", xn, xn_done, xnT_mm)
                if f:
                    second_product("F", 1, 1)
                if b:
                    max_transpose(0)
                if a:
                    pe.wait_ge(xnT_lo_done, st.count("A", 1, 1))
                    project("q", "wq", xnT_hi, xnT_lo, q_mm)
                    pe.wait_ge(ctx_lo_done, st.count("A", 1, 1))
                    project("k", "wk", ctx_hi, ctx_lo, k_mm)
                if b:
                    shifted_scores(0)
                if g:
                    if st.k == LAG["G"]:
                        pe.wait_ge(w_split, 6)
                    first_product(0)
                    first_product(1)
                if b:
                    attend(0)
                    plain_scores(1)
                if g:
                    first_product(2)
                    first_product(3)
                if a:
                    rows_out("v", (ctx_hi, ctx_lo), "wv", v_mm)
                if b:
                    max_transpose(1)
                if c:
                    if st.k == LAG["C"]:
                        pe.wait_ge(w_split, 6)
                    pe.wait_ge(attn_split, st.count("C", 2, 2))
                    rows_out("o", (attn_hi, attn_lo), "wo", o_mm)
                if g:
                    second_product("G", 0, 0)
                if b:
                    shifted_scores(1)
                if g:
                    second_product("G", 0, 1)
                if b:
                    attend(1)

            over_steps(pe, run_step)


_INS = ["x", "ctx_t", "mask", "wq", "wk", "wv", "wo", "w1", "w2", "bq", "bk", "bv", "bo", "b1", "b2"]


def kernel(**inputs):
    import concourse.bacc as bacc
    from concourse.bass_utils import run_bass_kernel_spmd

    n = {k.replace("L0_xattn_", "").replace("L0_ffn_", ""): np.asarray(v) for k, v in inputs.items()}

    def tiles(w):
        return w.reshape(w.shape[0] // P, P, w.shape[1]).transpose(1, 0, 2).reshape(P, -1)

    def by_dim(w):
        return w.reshape(w.shape[0], HH, KT, D).transpose(0, 2, 3, 1).reshape(w.shape[0], E)

    wo = n["Wo"].reshape(2, KT, 4, D, E).transpose(1, 2, 3, 0, 4).reshape(E, E)
    arrays = {
        "x": n["x"],
        "ctx_t": n["ctx_1024"].reshape(GROUPS, GB, S, KT, P).transpose(0, 4, 3, 1, 2).reshape(GROUPS, P, KT, T),
        "mask": n["mask_Bx1x1xS2_if1"],
        "wq": tiles(by_dim(n["Wq"])), "wk": tiles(by_dim(n["Wk"])), "wv": tiles(n["Wv"]), "wo": tiles(wo),
        "w1": tiles(n["W1"]), "w2": tiles(n["W2"]),
        "bq": by_dim(n["bq"][None]).reshape(KT, P).T, "bk": by_dim(n["bk"][None]).reshape(KT, P).T,
        "bv": n["bv"][None], "bo": n["bo"][None], "b1": n["b1"].reshape(FT, P).T, "b2": n["b2"][None],
    }
    arrays = {k: np.ascontiguousarray(v) for k, v in arrays.items()}
    nc = bacc.Bacc("TRN2", target_bir_lowering=False, num_devices=1)
    args = [nc.dram_tensor(f"in_{k}", arrays[k].shape, mybir.dt.from_np(arrays[k].dtype), kind="ExternalInput").ap()
            for k in _INS]
    out = nc.dram_tensor("out", (B, S, E), mybir.dt.float32, kind="ExternalOutput").ap()
    build(nc, *args, out)
    r = run_bass_kernel_spmd(nc, [{f"in_{k}": arrays[k] for k in _INS}], core_ids=[0])
    return r.results[0]["out"]
```

```python
import numpy as np
import concourse.bass as bass
from concourse import mybir
from contextlib import ExitStack


B, S, E, HEADS, F = 64, 128, 256, 16, 1024
D = E // HEADS
P = 128
GB = 2
T = GB * S
GROUPS = B // GB
KT = E // P
FT = F // P
HH = P // D
QUADS = HEADS // 4
EPS = 1e-5
MASKED = float(np.float32(-1e20))
SCORE_SCALE = 1.0 / float(np.sqrt(D))
PAIRS = ((0, 0), (0, 1), (1, 0), (0, 2), (1, 1), (2, 0))
ROWS_PRODUCTS = len(PAIRS) * D
ROWS_MASK = ROWS_PRODUCTS + 3
ROWS_MAX = ROWS_MASK + 3
PAIR_OF_ONES = float(np.array([0x3F803F80], np.uint32).view(np.float32)[0])


def stage_lags():
    return {"N": 0, "A": 1, "B": 2, "C": 3, "G": 4, "F": 5}


LAG = stage_lags()


class Step:

    def __init__(self, pair, k, in_loop):
        self.pair, self.k, self.in_loop = pair, k, in_loop

    def has(self, stage):
        return self.in_loop or 0 <= self.k - LAG[stage] < GROUPS

    def before(self):
        return Step(self.pair, self.k - 1, self.in_loop)

    def parity(self, stage):
        return (self.k - LAG[stage]) % 2

    def group(self, stage):
        return self.pair * 2 + (self.k - LAG[stage])

    def count(self, stage, per, done):
        return self.pair * (2 * per) + (per * (self.k - LAG[stage]) + done)

    def count_alternate(self, stage, per, done):
        return self.pair * per + (per * ((self.k - LAG[stage]) // 2) + done)


def split3(value):
    parts, rest = [], np.float32(value)
    for _ in range(3):
        bits = np.array(rest, np.float32).view(np.uint32).astype(np.uint64)
        bits = ((bits + 0x7FFF + ((bits >> 16) & 1)) & 0xFFFF0000).astype(np.uint32)
        part = bits.view(np.float32)
        parts.append(float(part))
        rest = np.float32(rest - part)
    return parts


def build(nc, x, ctx_t, mask, wq, wk, wv, wo, w1, w2, bq, bk, bv, bo, b1, b2, out):
    fp32, f32r, bf16, i32 = mybir.dt.float32, mybir.dt.float32r, mybir.dt.bfloat16, mybir.dt.int32
    ALU, ACT, AX = mybir.AluOpType, mybir.ActivationFunctionType, mybir.AxisListType

    x_g = x.rearrange("(g j) p e -> g p j e", j=GB)
    out_g = out.rearrange("(g j) p e -> g p j e", j=GB)
    mask_g = mask.rearrange("(g j) a b k -> g (a b) (j k)", j=GB)

    ctx = ExitStack()
    with ctx:
        def sb(name, shape, dt=fp32):
            return ctx.enter_context(nc.sbuf_tensor(name, shape, dt))

        def sem(name):
            return ctx.enter_context(nc.semaphore(name))

        w_cols = {"wq": KT * E, "wk": KT * E, "wv": KT * E, "wo": KT * E, "w1": KT * F, "w2": FT * E}
        w_at = {n: sum(list(w_cols.values())[:i]) for i, n in enumerate(w_cols)}
        w_raw = sb("w_raw", [P, sum(w_cols.values())])
        w_hi = {n: sb(f"{n}_hi", [P, c], f32r) for n, c in w_cols.items()}
        w_lo = {n: sb(f"{n}_lo", [P, c], f32r) for n, c in w_cols.items()}
        bq_col, bk_col, b1_col = sb("bq_col", [P, KT]), sb("bk_col", [P, KT]), sb("b1_col", [P, FT])
        bv_row, bo_row, b2_row = sb("bv_row", [P, 1, E]), sb("bo_row", [P, 1, E]), sb("b2_row", [P, 1, E])
        ident = sb("ident", [P, P])
        ident_bf = sb("ident_bf", [P, P], bf16)
        minus_half = sb("minus_half", [P, GB])

        x_in = [sb(f"x_in{i}", [P, GB, E]) for i in range(2)]
        n_stats, n_mv = sb("n_stats", [P, GB, 6]), sb("n_mv", [P, GB, 2])
        n_var, n_rstd = sb("n_var", [P, GB]), sb("n_rstd", [P, GB])
        xn = sb("xn", [P, GB, E])
        ctx_in = [sb(f"ctx_in{i}", [P, KT, T]) for i in range(2)]
        mask_in = [sb(f"mask_in{i}", [P, T], i32) for i in range(2)]
        keep = sb("keep", [P, T])
        mask_parts, masked_part = sb("mask_parts", [3, T], bf16), sb("masked_part", [3, 1])
        ctx_hi, ctx_lo = sb("ctx_hi", [P, KT, T], f32r), sb("ctx_lo", [P, KT, T], f32r)
        xnT_hi, xnT_lo = sb("xnT_hi", [P, KT, T], f32r), sb("xnT_lo", [P, KT, T], f32r)
        q_rest, k_rest = sb("q_rest", [P, KT, T]), sb("k_rest", [P, KT, T])
        q_parts, k_parts = sb("q_parts", [P, 3, KT, T], bf16), sb("k_parts", [P, 3, KT, T], bf16)
        q_rows = [sb(f"q_rows{i}", [P, HEADS, T], bf16) for i in range(2)]
        k_rows = [sb(f"k_rows{i}", [P, HEADS, T], bf16) for i in range(2)]
        v_ones = [sb(f"v_ones{i}", [P, GB, HEADS, D, 2]) for i in range(2)]
        minus_max, max_rest = sb("minus_max", [P, HEADS]), sb("max_rest", [P, HEADS])
        max_parts = sb("max_parts", [P, 3, HEADS], bf16)
        max_rows = sb("max_rows", [3 * HEADS, S], bf16)
        probs = sb("probs", [P, HEADS, S])
        attn_raw = sb("attn_raw", [P, QUADS, T])
        numer, denom = sb("numer", [P, KT, T]), sb("denom", [P, KT, T])
        attn_hi, attn_lo = sb("attn_hi", [P, KT, T], f32r), sb("attn_lo", [P, KT, T], f32r)
        x_res, x2 = sb("x_res", [P, GB, E]), sb("x2", [P, GB, E])
        x2_bias = [sb(f"x2_bias{i}", [P, GB, E]) for i in range(2)]
        c_stats, c_mv = sb("c_stats", [P, GB, 6]), sb("c_mv", [P, GB, 2])
        c_var, c_rstd = sb("c_var", [P, GB]), sb("c_rstd", [P, GB])
        x2n = sb("x2n", [P, GB, E])
        x2T_hi, x2T_lo = sb("x2T_hi", [P, KT, T], f32r), sb("x2T_lo", [P, KT, T], f32r)
        hid = [sb(f"hid{i}", [P, 2, T]) for i in range(3)]
        hid_hi, hid_lo = sb("hid_hi", [P, FT, T], f32r), sb("hid_lo", [P, FT, T], f32r)

        scores = [ctx.enter_context(nc.psum_tensor(f"scores{i}", [P, HEADS // 2, S], fp32)) for i in range(2)]
        attn_ps = ctx.enter_context(nc.psum_tensor("attn_ps", [P, QUADS, S], fp32))
        bank = {n: ctx.enter_context(nc.psum_tensor(f"bank_{n}", [P, 2, T], fp32)) for n in "ABC"}
        max_ps = attn_ps[:, :, :].rearrange("p a b -> p (a b)").bitcast(bf16)[0:3 * HEADS, 0:S]

        w_loaded = {n: sem(f"{n}_loaded") for n in w_cols}
        consts_loaded, w_split_hi, w_split = sem("consts_loaded"), sem("w_split_hi"), sem("w_split")
        ident_zeroed, consts_set, masked_set = sem("ident_zeroed"), sem("consts_set"), sem("masked_set")
        q_rows_set, k_rows_set, v_ones_set = sem("q_rows_set"), sem("k_rows_set"), sem("v_ones_set")
        x_loaded, ctx_loaded = [sem("x_loaded0"), sem("x_loaded1")], [sem("ctx_loaded0"), sem("ctx_loaded1")]
        mask_loaded = [sem("mask_loaded0"), sem("mask_loaded1")]
        res_loaded, out_stored = sem("res_loaded"), [sem("out_stored0"), sem("out_stored1")]
        n_bn, n_ag, n_var_done, n_pow = sem("n_bn"), sem("n_ag"), sem("n_var_done"), sem("n_pow")
        xn_done, xnT_mm, xnT_hi_done, xnT_lo_done = sem("xn_done"), sem("xnT_mm"), sem("xnT_hi_done"), sem("xnT_lo_done")
        keep_done, mask_parts_done = sem("keep_done"), sem("mask_parts_done")
        ctx_hi_done, ctx_lo_done = sem("ctx_hi_done"), sem("ctx_lo_done")
        q_mm, k_mm, v_mm = sem("q_mm"), sem("k_mm"), sem("v_mm")
        q_out, k_out, q_hi_done, k_hi_done = sem("q_out"), sem("k_out"), sem("q_hi_done"), sem("k_hi_done")
        q_split, k_split, v_done = sem("q_split"), sem("k_split"), sem("v_done")
        q_rows_in, k_rows_in = [sem("q_rows_in0"), sem("q_rows_in1")], [sem("k_rows_in0"), sem("k_rows_in1")]
        scores_mm, max_done, max_split, maxT_mm, max_rows_done = sem("scores_mm"), sem("max_done"), sem("max_split"), sem("maxT_mm"), sem("max_rows_done")
        max_rows_in, shifted_mm, probs_done, attn_mm, attn_out = sem("max_rows_in"), sem("shifted_mm"), sem("probs_done"), sem("attn_mm"), sem("attn_out")
        packed = sem("packed")
        recip_done, attn_norm, attn_split, o_mm = sem("recip_done"), sem("attn_norm"), sem("attn_split"), sem("o_mm")
        res_bias, x2_done, x2_bias_done = sem("res_bias"), sem("x2_done"), sem("x2_bias_done")
        c_bn, c_ag, c_var_done, c_pow = sem("c_bn"), sem("c_ag"), sem("c_var_done"), sem("c_pow")
        x2n_done, x2T_mm, x2T_hi_done, x2T_lo_done = sem("x2n_done"), sem("x2T_mm"), sem("x2T_hi_done"), sem("x2T_lo_done")
        hid_mm, hid_out, hid_hi_done, hid_lo_done = sem("hid_mm"), sem("hid_out"), sem("hid_hi_done"), sem("hid_lo_done")
        f_mm, y_done = sem("f_mm"), sem("y_done")
        act_passed, sp_passed, pool_passed, dve_passed, pe_passed = sem("act_passed"), sem("sp_passed"), sem("pool_passed"), sem("dve_passed"), sem("pe_passed")

        def alone(eng, passed, semaphore, value):
            if isinstance(value, int):
                if value > 0:
                    eng.wait_ge(semaphore, value)
            else:
                eng.wait_ge(semaphore, value)
                eng.sem_inc(passed, 1)

        FILLS = [("xnT", "A", "C", xnT_lo_done, 1), ("q", "A", "B", q_out, 1), ("x2T", "G", "A", x2T_lo_done, 1),
                 ("k", "A", "C", k_out, 1), ("h0", "G", "B", hid_out, 4), ("h1", "G", "C", hid_out, 4),
                 ("h2", "G", "A", hid_out, 4), ("h3", "G", "B", hid_out, 4), ("v", "A", "C", v_done, 1),
                 ("f", "G", "A", y_done, 1), ("o", "C", "B", x2_done, 1)]
        BANK_OF = {name: bank[b] for name, _, b, _, _ in FILLS}

        def bank_free(eng, st, name):
            names = [f[0] for f in FILLS]
            me = FILLS[names.index(name)]
            here = [(st, f) for f in FILLS[:names.index(name)] if f[2] == me[2] and st.has(f[1])]
            prev, back = st, []
            while not here and not back:
                prev = prev.before()
                if not prev.in_loop and prev.k < 0:
                    return
                back = [(prev, f) for f in FILLS if f[2] == me[2] and prev.has(f[1])]
            at, f = (here or back)[-1]
            done = 1 if f[4] == 1 else int(f[0][1:]) + 1
            eng.wait_ge(f[3], at.count(f[1], f[4], done))

        def over_steps(eng, run_step):
            first = LAG["F"] + (GROUPS - LAG["F"]) % 2
            for k in range(first):
                run_step(Step(0, k, False))
            with eng.Fori(0, (GROUPS - first) // 2) as pair:
                run_step(Step(pair, first, True))
                run_step(Step(pair, first + 1, True))
            for k in range(GROUPS, GROUPS + LAG["F"]):
                run_step(Step(0, k, False))

        block = ctx.enter_context(nc.Block())

        @block.sync
        def _(sp):
            def load_weights(*names):
                for n in names:
                    w = {"wq": wq, "wk": wk, "wv": wv, "wo": wo, "w1": w1, "w2": w2}[n]
                    sp.dma_start(w_raw[:, w_at[n]:w_at[n] + w_cols[n]], w).then_inc(w_loaded[n], 16)

            def load_group(st):
                group, par = st.group("N"), st.parity("N")
                if st.in_loop or st.k > 1:
                    alone(sp, sp_passed, xn_done, st.count("A", GB, 0))
                    alone(sp, sp_passed, ctx_lo_done, st.count("A", 1, 0))
                    alone(sp, sp_passed, keep_done, st.count("A", 1, 0))
                    alone(sp, sp_passed, mask_parts_done, st.count("A", 1, 0))
                sp.dma_start(x_in[par][:, :, :], x_g[group]).then_inc(x_loaded[par], 16)
                if st.k == 0:
                    load_weights("wq", "wk")
                sp.dma_start(ctx_in[par][:, :, :], ctx_t[group]).then_inc(ctx_loaded[par], 16)
                sp.dma_start(mask_in[par][:, :], mask_g[group].to_broadcast((P, T))).then_inc(mask_loaded[par], 16)

            load_group(Step(0, 0, False))
            for t, v in ((bq_col, bq), (bk_col, bk), (b1_col, b1)):
                sp.dma_start(t[:, :], v).then_inc(consts_loaded, 16)
            for t, v in ((bv_row, bv), (bo_row, bo), (b2_row, b2)):
                sp.dma_start(t[:, 0, :], v.to_broadcast((P, E))).then_inc(consts_loaded, 16)
            load_weights("wv", "wo")

            def run_step(st):
                if st.has("N") and (st.in_loop or st.k > 0):
                    load_group(st)
                if st.k == 1:
                    load_weights("w1", "w2")
                if st.has("C"):
                    alone(sp, sp_passed, x2_done, st.count("C", 1, 0))
                    sp.dma_start(x_res[:, :, :], x_g[st.group("C")]).then_inc(res_loaded, 16)
                    alone(sp, sp_passed, attn_out, st.count("C", GB, GB))
                    alone(sp, sp_passed, attn_split, st.count("C", 2, 0))
                    for half, dst in ((0, numer), (1, denom)):
                        sp.dma_start(dst[:, :, :], attn_raw[half::2, :, :]).then_inc(packed, 16)
                if st.has("F"):
                    alone(sp, sp_passed, y_done, st.count("F", 1, 1))
                    sp.dma_start(out_g[st.group("F")], x2_bias[st.parity("F")][:, :, :]).then_inc(out_stored[st.parity("F")], 16)
                if st.has("A"):
                    par = st.parity("A")
                    if st.in_loop or st.k > LAG["A"] + 1:
                        alone(sp, sp_passed, shifted_mm, st.count("B", 2 * GB, 0))
                    alone(sp, sp_passed, mask_parts_done, st.count("A", 1, 1))
                    if st.k <= LAG["A"] + 1:
                        sp.wait_ge(k_rows_set, st.k)
                        sp.wait_ge(q_rows_set, st.k)
                    sp.dma_start(k_rows[par][ROWS_PRODUCTS:ROWS_MASK, :, :],
                                 mask_parts[:, :].unsqueeze(1).to_broadcast((3, HEADS, T))).then_inc(k_rows_in[par], 16)
                    for which, rows, parts, rows_in, hi_done, split in (
                            (0, q_rows, q_parts, q_rows_in, q_hi_done, q_split), (1, k_rows, k_parts, k_rows_in, k_hi_done, k_split)):
                        for part in range(3):
                            if part == 0:
                                alone(sp, sp_passed, hi_done, st.count("A", 1, 1))
                            else:
                                alone(sp, sp_passed, split, st.count("A", 3, part + 1))
                            for n in [n for n, pair in enumerate(PAIRS) if pair[which] == part]:
                                sp.dma_start(rows[par][n * D:(n + 1) * D, :, :].rearrange("d h t -> d (h t)"),
                                             parts[:, part, :, :].rearrange("p a t -> p (a t)")).then_inc(rows_in[par], 16)

            over_steps(sp, run_step)
            for stored in out_stored:
                sp.wait_ge(stored, 16 * GROUPS // 2)

        @block.gpsimd
        def _(pool):
            for t in (ident, ident_bf):
                nc.gpsimd.memset(t[:, :], 0.0).then_inc(ident_zeroed, 1)
            pool.wait_ge(ident_zeroed, 2)
            for t in (ident, ident_bf):
                nc.gpsimd.affine_select(out=t[:, :], in_=t[:, :], compare_op=ALU.not_equal, fill=1.0, base=0,
                                        pattern=[[-1, P]], channel_multiplier=1).then_inc(consts_set, 1)
            nc.gpsimd.memset(minus_half[:, :], -0.5).then_inc(consts_set, 1)
            pool.wait_ge(consts_set, 3)

            def set_ones(i):
                nc.gpsimd.memset(k_rows[i][ROWS_PRODUCTS:P, :, :].bitcast(fp32), PAIR_OF_ONES).then_inc(k_rows_set, 1)
                pool.wait_ge(k_rows_set, i + 1)
                nc.gpsimd.memset(v_ones[i][:, :, :, :, :], 1.0).then_inc(v_ones_set, 1)
                pool.wait_ge(v_ones_set, i + 1)

            set_ones(0)

            def split_in_three(st, hi_done, done, parts, rest):
                alone(pool, pool_passed, hi_done, st.count("A", 1, 1))
                nc.gpsimd.tensor_tensor(rest[:, :, :], rest[:, :, :], parts[:, 0, :, :], ALU.subtract).then_inc(done, 1)
                alone(pool, pool_passed, done, st.count("A", 3, 1))
                nc.gpsimd.tensor_scalar(parts[:, 1, :, :], rest[:, :, :], 1.0, 1.0, ALU.mult, ALU.mult).then_inc(done, 1)
                alone(pool, pool_passed, done, st.count("A", 3, 2))
                nc.gpsimd.tensor_tensor(parts[:, 2, :, :], rest[:, :, :], parts[:, 1, :, :], ALU.subtract).then_inc(done, 1)

            def run_step(st):
                if st.has("C"):
                    alone(pool, pool_passed, res_loaded, st.count("C", 16, 16))
                    if st.k == LAG["C"]:
                        pool.wait_ge(consts_loaded, 6 * 16)
                    nc.gpsimd.tensor_tensor(x_res[:, :, :], x_res[:, :, :], bo_row[:, :, :].to_broadcast((P, GB, E)),
                                            ALU.add).then_inc(res_bias, 1)
                if st.has("A"):
                    split_in_three(st, q_hi_done, q_split, q_parts, q_rest)
                    if st.k > LAG["A"]:
                        split_in_three(st, k_hi_done, k_split, k_parts, k_rest)
                if st.has("C"):
                    alone(pool, pool_passed, recip_done, st.count("C", 2, 2))
                    nc.gpsimd.tensor_tensor(numer[:, :, :], numer[:, :, :], denom[:, :, :], ALU.mult).then_inc(attn_norm, 1)
                    alone(pool, pool_passed, attn_norm, st.count("C", 1, 1))
                    alone(pool, pool_passed, o_mm, st.count("C", 1, 0))
                    nc.gpsimd.tensor_scalar(attn_hi[:, :, :], numer[:, :, :], 1.0, 1.0, ALU.mult,
                                            ALU.mult).then_inc(attn_split, 1)
                    alone(pool, pool_passed, attn_split, st.count("C", 2, 1))
                    nc.gpsimd.tensor_tensor(attn_lo[:, :, :], numer[:, :, :], attn_hi[:, :, :].bitcast(fp32),
                                            ALU.subtract).then_inc(attn_split, 1)
                if st.has("N"):
                    alone(pool, pool_passed, n_var_done, st.count("N", 1, 1))
                    nc.gpsimd.tensor_tensor(n_rstd[:, :], n_var[:, :], minus_half[:, :], ALU.pow).then_inc(n_pow, 1)
                    par = st.parity("N")
                    alone(pool, pool_passed, ctx_loaded[par], st.count_alternate("N", 16, 16))
                    alone(pool, pool_passed, v_mm, st.count("N", 1, 0))
                    nc.gpsimd.tensor_scalar(ctx_hi[:, :, :], ctx_in[par][:, :, :], 1.0, 1.0, ALU.mult,
                                            ALU.mult).then_inc(ctx_hi_done, 1)
                    alone(pool, pool_passed, ctx_hi_done, st.count("N", 1, 1))
                    nc.gpsimd.tensor_tensor(ctx_lo[:, :, :], ctx_in[par][:, :, :], ctx_hi[:, :, :].bitcast(fp32),
                                            ALU.subtract).then_inc(ctx_lo_done, 1)
                if st.k == 0:
                    pool.wait_ge(ctx_lo_done, 1)
                    set_ones(1)
                if st.has("C"):
                    alone(pool, pool_passed, c_var_done, st.count("C", 1, 1))
                    nc.gpsimd.tensor_tensor(c_rstd[:, :], c_var[:, :], minus_half[:, :], ALU.pow).then_inc(c_pow, 1)
                    if st.has("F"):
                        alone(pool, pool_passed, out_stored[st.parity("F")], st.count_alternate("F", 16, 16))
                    nc.gpsimd.tensor_tensor(x2_bias[st.parity("C")][:, :, :], x2[:, :, :],
                                            b2_row[:, :, :].to_broadcast((P, GB, E)), ALU.add).then_inc(x2_bias_done, 1)

            over_steps(pool, run_step)

        @block.scalar
        def _(act):
            def weights_hi(*names):
                for n in names:
                    act.wait_ge(w_loaded[n], 16)
                    nc.scalar.activation(w_hi[n][:, :], w_raw[:, w_at[n]:w_at[n] + w_cols[n]], ACT.Copy).then_inc(w_split_hi, 1)

            weights_hi("wq", "wk")

            def run_step(st):
                def transposed_hi(stage, name, mm, hi, done, used, used_count):
                    alone(act, act_passed, mm, st.count(stage, 1, 1))
                    alone(act, act_passed, used, used_count)
                    nc.scalar.activation(hi[:, :, :], BANK_OF[name][:, :, :], ACT.Copy).then_inc(done, 1)

                def max_rows_out(j):
                    alone(act, act_passed, maxT_mm, st.count("B", GB, j + 1))
                    alone(act, act_passed, max_rows_in, st.count("B", 16 * GB, 16 * j))
                    nc.scalar.activation(max_rows[:, :], max_ps, ACT.Copy).then_inc(max_rows_done, 1)

                def max_rows_move(j):
                    alone(act, act_passed, max_rows_done, st.count("B", GB, j + 1))
                    act.dma_start(q_rows[st.parity("B")][ROWS_MASK:ROWS_MAX, :, j * S:(j + 1) * S],
                                  max_rows[:, :]).then_inc(max_rows_in, 16)

                def exps(j, half):
                    alone(act, act_passed, shifted_mm, st.count("B", 2 * GB, 2 * j + half + 1))
                    alone(act, act_passed, attn_mm, st.count("B", GB, j))
                    nc.scalar.activation(probs[:, half * 8:half * 8 + 8, :], scores[half][:, :, :], ACT.Exp,
                                         scale=SCORE_SCALE).then_inc(probs_done, 1)

                def attn_evac(stage, j):
                    alone(act, act_passed, attn_mm, st.count(stage, GB, j + 1))
                    if j == 0:
                        alone(act, act_passed, packed, st.count("B", 32, 0))
                    nc.scalar.activation(attn_raw[:, :, j * S:(j + 1) * S], attn_ps[:, :, :], ACT.Copy).then_inc(attn_out, 1)

                def hidden(i):
                    alone(act, act_passed, hid_mm, st.count("G", 4, i + 1))
                    if i in (0, 3):
                        alone(act, act_passed, hid_lo_done, st.count("G", 4, 0 if i == 0 else 1))
                    for u in range(2):
                        f = 2 * i + u
                        ins = nc.scalar.activation(hid[i % 3][:, u, :], BANK_OF[f"h{i}"][:, u, :], ACT.Relu,
                                                   bias=b1_col[:, f:f + 1])
                    ins.then_inc(hid_out, 1)

                def hidden_hi(i):
                    alone(act, act_passed, hid_out, st.count("G", 4, i + 1))
                    alone(act, act_passed, f_mm, st.count("G", 1, 0))
                    nc.scalar.activation(hid_hi[:, 2 * i:2 * i + 2, :], hid[i % 3][:, :, :], ACT.Copy).then_inc(hid_hi_done, 1)

                def queries_out():
                    if st.k == LAG["A"]:
                        act.wait_ge(consts_loaded, 6 * 16)
                    alone(act, act_passed, q_mm, st.count("A", 1, 1))
                    alone(act, act_passed, q_split, st.count("A", 3, 0))
                    for t in range(KT):
                        ins = nc.scalar.activation(q_rest[:, t, :], BANK_OF["q"][:, t, :], ACT.Identity, bias=bq_col[:, t:t + 1])
                    ins.then_inc(q_out, 1)

                def queries_top():
                    alone(act, act_passed, q_out, st.count("A", 1, 1))
                    top_part(q_rest, q_parts, q_rows_in, 96, q_hi_done)

                def top_part(rest, parts, rows_in, per, done):
                    if st.in_loop or st.k > LAG["A"]:
                        last = st.before()
                        alone(act, act_passed, rows_in[last.parity("A")], last.count_alternate("A", per, per))
                    nc.scalar.activation(parts[:, 0, :, :], rest[:, :, :], ACT.Copy).then_inc(done, 1)

                if st.has("C"):
                    attn_evac("C", 1)
                if st.has("A"):
                    transposed_hi("A", "xnT", xnT_mm, xnT_hi, xnT_hi_done, q_mm, st.count("A", 1, 0))
                if st.has("B"):
                    max_rows_out(0)
                    max_rows_move(0)
                if st.k == LAG["A"]:
                    weights_hi("wv", "wo")
                if st.has("A"):
                    queries_out()
                if st.has("G"):
                    transposed_hi("G", "x2T", x2T_mm, x2T_hi, x2T_hi_done, hid_mm, st.count("G", 4, 0))
                if st.has("A"):
                    queries_top()
                if st.has("B"):
                    exps(0, 0)
                if st.has("A"):
                    alone(act, act_passed, k_out, st.count("A", 1, 1))
                    top_part(k_rest, k_parts, k_rows_in, 112, k_hi_done)
                if st.k == LAG["A"]:
                    weights_hi("w1", "w2")
                if st.has("B"):
                    exps(0, 1)
                if st.has("G"):
                    hidden(0)
                    hidden_hi(0)
                    hidden(1)
                    hidden_hi(1)
                if st.has("B"):
                    attn_evac("B", 0)
                if st.has("G"):
                    hidden(2)
                    hidden_hi(2)
                if st.has("B"):
                    max_rows_out(1)
                if st.has("G"):
                    hidden(3)
                if st.has("B"):
                    max_rows_move(1)
                if st.has("G"):
                    hidden_hi(3)
                if st.has("B"):
                    exps(1, 0)
                    exps(1, 1)

            over_steps(act, run_step)

        @block.vector
        def _(dve):
            for n, r in enumerate((2, 1, 0)):
                if n:
                    dve.wait_ge(masked_set, n)
                nc.vector.memset(masked_part[0:r + 1, :], split3(MASKED)[r]).then_inc(masked_set, 1)
            dve.wait_ge(masked_set, 3)

            def set_query_ones(i):
                nc.vector.memset(q_rows[i][ROWS_PRODUCTS:P, :, :].bitcast(fp32), PAIR_OF_ONES).then_inc(q_rows_set, 1)

            def weights_lo(*names):
                for n in names:
                    raw = w_raw[:, w_at[n]:w_at[n] + w_cols[n]]
                    dve.wait_ge(w_split_hi, list(w_cols).index(n) + 1)
                    nc.vector.tensor_tensor(w_lo[n][:, :], raw, w_hi[n][:, :].bitcast(fp32), ALU.subtract).then_inc(w_split, 1)

            def run_step(st):
                def statistics(stage, src, stats, mv, var, bn, ag, var_done):
                    for j in range(GB):
                        nc.vector.bn_stats(stats[:, j, :], src[:, j, :]).then_inc(bn, 1)
                    for j in range(GB):
                        alone(dve, dve_passed, bn, st.count(stage, GB, GB))
                        nc.vector.bn_aggr(mv[:, j, :], stats[:, j, :]).then_inc(ag, 1)
                    dve.wait_ge(ag, st.count(stage, GB, GB))
                    nc.vector.tensor_scalar_add(var[:, :], mv[:, :, 1], EPS).then_inc(var_done, 1)

                def normalise(stage, src, mv, rstd, pow_done, dst, done):
                    alone(dve, dve_passed, pow_done, st.count(stage, 1, 1))
                    for j in range(GB):
                        nc.vector.tensor_scalar(dst[:, j, :], src[:, j, :], mv[:, j, 0:1], rstd[:, j:j + 1],
                                                ALU.subtract, ALU.mult).then_inc(done, 1)

                def maxima(j):
                    for half in range(2):
                        alone(dve, dve_passed, scores_mm, st.count("B", 2 * GB, 2 * j + half + 1))
                        nc.vector.tensor_reduce(minus_max[:, half * 8:half * 8 + 8], scores[half][:, :, :], axis=AX.X,
                                                op=ALU.max, negate=True).then_inc(max_done, 1)
                    alone(dve, dve_passed, max_done, st.count("B", 2 * GB, 2 * j + 2))
                    alone(dve, dve_passed, maxT_mm, st.count("B", GB, j))
                    nc.vector.tensor_copy(max_parts[:, 0, :], minus_max[:, :]).then_inc(max_split, 1)
                    dve.wait_ge(max_split, st.count("B", 4 * GB, 4 * j + 1))
                    nc.vector.tensor_tensor(max_rest[:, :], minus_max[:, :], max_parts[:, 0, :], ALU.subtract).then_inc(max_split, 1)
                    dve.wait_ge(max_split, st.count("B", 4 * GB, 4 * j + 2))
                    nc.vector.tensor_copy(max_parts[:, 1, :], max_rest[:, :]).then_inc(max_split, 1)
                    dve.wait_ge(max_split, st.count("B", 4 * GB, 4 * j + 3))
                    nc.vector.tensor_tensor(max_parts[:, 2, :], max_rest[:, :], max_parts[:, 1, :], ALU.subtract).then_inc(max_split, 1)

                def transposed_lo(stage, name, hi, lo, hi_done, done):
                    alone(dve, dve_passed, hi_done, st.count(stage, 1, 1))
                    nc.vector.tensor_tensor(lo[:, :, :], BANK_OF[name][:, :, :], hi[:, :, :].bitcast(fp32),
                                            ALU.subtract).then_inc(done, 1)

                def hidden_lo(i):
                    alone(dve, dve_passed, hid_hi_done, st.count("G", 4, i + 1))
                    nc.vector.tensor_tensor(hid_lo[:, 2 * i:2 * i + 2, :], hid[i % 3][:, :, :],
                                            hid_hi[:, 2 * i:2 * i + 2, :].bitcast(fp32), ALU.subtract).then_inc(hid_lo_done, 1)

                def mask_out():
                    par = st.parity("A")
                    alone(dve, dve_passed, mask_loaded[par], st.count_alternate("A", 16, 16))
                    nc.vector.tensor_scalar(keep[:, :], mask_in[par][:, :], 0.0, None, ALU.not_equal).then_inc(keep_done, 1)
                    if st.in_loop or st.k > LAG["A"]:
                        last = st.before()
                        alone(dve, dve_passed, k_rows_in[last.parity("A")], last.count_alternate("A", 112, 112))
                    nc.vector.tensor_scalar(mask_parts[:, :], mask_in[par][0:3, :], 0.0, masked_part[:, 0:1],
                                            ALU.is_equal, ALU.mult).then_inc(mask_parts_done, 1)

                def keys_out():
                    alone(dve, dve_passed, k_mm, st.count("A", 1, 1))
                    alone(dve, dve_passed, keep_done, st.count("A", 1, 1))
                    alone(dve, dve_passed, k_split, st.count("A", 3, 0))
                    if st.k == LAG["A"]:
                        dve.wait_ge(consts_loaded, 6 * 16)
                    for t in range(KT):
                        ins = nc.vector.scalar_tensor_tensor(out=k_rest[:, t, :], in0=BANK_OF["k"][:, t, :],
                                                             scalar=bk_col[:, t:t + 1], in1=keep[:, :],
                                                             op0=ALU.add, op1=ALU.mult)
                    ins.then_inc(k_out, 1)

                def first_keys_split():
                    dve.wait_ge(k_hi_done, 1)
                    nc.vector.tensor_tensor(k_rest[:, :, :], k_rest[:, :, :], k_parts[:, 0, :, :], ALU.subtract).then_inc(k_split, 1)
                    dve.wait_ge(k_split, 1)
                    nc.vector.tensor_copy(k_parts[:, 1, :, :], k_rest[:, :, :]).then_inc(k_split, 1)
                    dve.wait_ge(k_split, 2)
                    nc.vector.tensor_tensor(k_parts[:, 2, :, :], k_rest[:, :, :], k_parts[:, 1, :, :], ALU.subtract).then_inc(k_split, 1)

                def reciprocals(tile):
                    alone(dve, dve_passed, packed, st.count("C", 32, 32))
                    nc.vector.reciprocal(denom[:, tile, :], denom[:, tile, :]).then_inc(recip_done, 1)

                def values_out():
                    if st.k <= LAG["A"] + 1:
                        dve.wait_ge(v_ones_set, st.k)
                    alone(dve, dve_passed, v_mm, st.count("A", 1, 1))
                    for j in range(GB):
                        ins = nc.vector.tensor_tensor(
                            v_ones[st.parity("A")][:, j, :, :, 0], BANK_OF["v"][:, j, :].rearrange("p (h d) -> p h d", d=D),
                            bv_row[:, 0, :].rearrange("p (h d) -> p h d", d=D), ALU.add)
                    ins.then_inc(v_done, 1)

                if st.has("B"):
                    maxima(0)
                if st.has("A"):
                    transposed_lo("A", "xnT", xnT_hi, xnT_lo, xnT_hi_done, xnT_lo_done)
                if st.has("G"):
                    alone(dve, dve_passed, x2T_mm, st.count("G", 1, 0))
                    normalise("G", x2, c_mv, c_rstd, c_pow, x2n, x2n_done)
                if st.has("F"):
                    alone(dve, dve_passed, f_mm, st.count("F", 1, 1))
                    alone(dve, dve_passed, x2_bias_done, st.count("F", 1, 1))
                    y = x2_bias[st.parity("F")]
                    nc.vector.tensor_tensor(y[:, :, :], BANK_OF["f"][:, :, :], y[:, :, :], ALU.add).then_inc(y_done, 1)
                if st.has("A"):
                    mask_out()
                if st.has("C") and st.has("A"):
                    reciprocals(0)
                if st.has("G"):
                    transposed_lo("G", "x2T", x2T_hi, x2T_lo, x2T_hi_done, x2T_lo_done)
                if st.k == LAG["A"]:
                    weights_lo("wv")
                    set_query_ones(0)
                if st.k == LAG["B"]:
                    weights_lo("w1", "w2")
                if st.has("A"):
                    keys_out()
                if st.k == LAG["A"]:
                    first_keys_split()
                if st.has("C"):
                    if not st.has("A"):
                        reciprocals(0)
                    reciprocals(1)
                if st.has("N"):
                    par = st.parity("N")
                    alone(dve, dve_passed, x_loaded[par], st.count_alternate("N", 16, 16))
                    statistics("N", x_in[par], n_stats, n_mv, n_var, n_bn, n_ag, n_var_done)
                if st.has("B"):
                    maxima(1)
                if st.has("G"):
                    hidden_lo(0)
                    hidden_lo(1)
                    hidden_lo(2)
                if st.has("N"):
                    alone(dve, dve_passed, xnT_mm, st.count("N", 1, 0))
                    normalise("N", x_in[st.parity("N")], n_mv, n_rstd, n_pow, xn, xn_done)
                if st.has("G"):
                    hidden_lo(3)
                if st.has("A"):
                    values_out()
                if st.has("C"):
                    alone(dve, dve_passed, o_mm, st.count("C", 1, 1))
                    alone(dve, dve_passed, res_bias, st.count("C", 1, 1))
                    alone(dve, dve_passed, x2_bias_done, st.count("C", 1, 0))
                    nc.vector.tensor_tensor(x2[:, :, :], BANK_OF["o"][:, :, :], x_res[:, :, :], ALU.add).then_inc(x2_done, 1)
                    alone(dve, dve_passed, x2_done, st.count("C", 1, 1))
                    statistics("C", x2, c_stats, c_mv, c_var, c_bn, c_ag, c_var_done)
                if st.k == 0:
                    weights_lo("wq", "wk")
                if st.k == LAG["A"]:
                    set_query_ones(1)
                    weights_lo("wo")

            over_steps(dve, run_step)

        @block.tensor
        def _(pe):
            w = {n: (w_hi[n][:, :].rearrange("p (k m) -> p k m", k=KT if n != "w2" else FT),
                     w_lo[n][:, :].rearrange("p (k m) -> p k m", k=KT if n != "w2" else FT)) for n in w_cols}

            def three_passes(out_ap, lhs, rhs, steps, first=True, last=True):
                runs = [(a, b, k) for k in steps for a, b in ((1, 0), (0, 1), (0, 0))]
                for n, (a, b, k) in enumerate(runs):
                    ins = nc.tensor.matmul(out_ap, lhs(a, k), rhs(b, k), start=first and n == 0,
                                           stop=last and n == len(runs) - 1)
                return ins

            def run_step(st):
                def score_rows(j, rows, done, slot_free):
                    par = st.parity("B")
                    for half in range(2):
                        slot_free(half)
                        for i in range(8):
                            h = half * 8 + i
                            ks = k_rows[par][0:rows, h, j * S:(j + 1) * S]
                            qs = q_rows[par][0:rows, h, j * S:(j + 1) * S]
                            a, b = (qs, ks) if rows == ROWS_MASK else (ks, qs)
                            ins = nc.tensor.matmul(scores[half][:, i, :], a, b, start=True, stop=True)
                        ins.then_inc(done, 1)

                def plain_scores(j):
                    if j == 0:
                        par = st.parity("B")
                        pe.wait_ge(q_rows_in[par], st.count_alternate("B", 96, 96))
                        pe.wait_ge(k_rows_in[par], st.count_alternate("B", 112, 112))

                    def slot_free(half):
                        if st.in_loop or st.k > LAG["B"] or j > 0:
                            pe.wait_ge(probs_done, st.count("B", 2 * GB, 2 * j - 1 + half))
                    score_rows(j, ROWS_MASK, scores_mm, slot_free)

                def max_transpose(j):
                    alone(pe, pe_passed, max_split, st.count("B", 4 * GB, 4 * j + 4))
                    alone(pe, pe_passed, attn_out, st.count("B", GB, j))
                    nc.tensor.transpose(max_ps, max_parts[:, :, :].rearrange("p a h -> p (a h)"),
                                        ident_bf[:, :]).then_inc(maxT_mm, 1)

                def shifted_scores(j):
                    pe.wait_ge(max_rows_in, st.count("B", 16 * GB, 16 * (j + 1)))

                    def slot_free(half):
                        pe.wait_ge(max_done, st.count("B", 2 * GB, 2 * j + half + 1))
                    score_rows(j, ROWS_MAX, shifted_mm, slot_free)

                def attend(stage, j):
                    par = st.parity(stage)
                    pe.wait_ge(probs_done, st.count(stage, 2 * GB, 2 * j + 2))
                    pe.wait_ge(v_done, st.count(stage, 1, 1))
                    for quad in range(QUADS):
                        for r in range(4):
                            h = 4 * quad + r
                            ins = nc.tensor.matmul(attn_ps[32 * r:32 * r + 32, quad, :],
                                                   v_ones[par][:, j, h, :, :].rearrange("p d a -> p (d a)"),
                                                   probs[:, h, :], start=True, stop=True)
                    ins.then_inc(attn_mm, 1)

                def transposes(stage, name, src, src_done, mm):
                    bank_free(pe, st, name)
                    pe.wait_ge(src_done, st.count(stage, GB, GB))
                    for t in range(KT):
                        for j in range(GB):
                            ins = nc.tensor.transpose(BANK_OF[name][:, t, j * S:(j + 1) * S],
                                                      src[:, j, t * P:(t + 1) * P], ident[:, :])
                    ins.then_inc(mm, 1)

                def project(name, w_name, hi, lo, mm):
                    bank_free(pe, st, name)
                    for t in range(KT):
                        ins = three_passes(BANK_OF[name][:, t, :],
                                           lambda a, k: w[w_name][a][:, k, t * P:(t + 1) * P],
                                           lambda b, k: (hi, lo)[b][:, k, :], range(KT))
                    ins.then_inc(mm, 1)

                def rows_out(name, pair, w_name, mm):
                    bank_free(pe, st, name)
                    for j in range(GB):
                        ins = three_passes(BANK_OF[name][:, j, :],
                                           lambda a, k: pair[a][:, k, j * S:(j + 1) * S],
                                           lambda b, k: w[w_name][b][:, k, :], range(KT))
                    ins.then_inc(mm, 1)

                def second_product(stage, j, half):
                    steps = range(half * FT // 2, (half + 1) * FT // 2)
                    if j == 0:
                        if half == 0:
                            bank_free(pe, st, "f")
                        pe.wait_ge(hid_lo_done, st.count(stage, 4, 2 * half + 2))
                    ins = three_passes(BANK_OF["f"][:, j, :], lambda a, k: (hid_hi, hid_lo)[a][:, k, j * S:(j + 1) * S],
                                       lambda b, k: w["w2"][b][:, k, :], steps, half == 0, half == 1)
                    if j == GB - 1 and half == 1:
                        ins.then_inc(f_mm, 1)

                def first_product(i):
                    bank_free(pe, st, f"h{i}")
                    if i == 0:
                        pe.wait_ge(x2T_lo_done, st.count("G", 1, 1))
                    for u in range(2):
                        f = 2 * i + u
                        ins = three_passes(BANK_OF[f"h{i}"][:, u, :], lambda a, k: w["w1"][a][:, k, f * P:(f + 1) * P],
                                           lambda b, k: (x2T_hi, x2T_lo)[b][:, k, :], range(KT))
                    ins.then_inc(hid_mm, 1)

                a, b, c, g, f = st.has("A"), st.has("B"), st.has("C"), st.has("G"), st.has("F")
                if b:
                    plain_scores(0)
                if c:
                    attend("C", 1)
                if a:
                    if st.k == LAG["A"]:
                        pe.wait_ge(consts_set, 3)
                    transposes("A", "xnT", xn, xn_done, xnT_mm)
                if f:
                    second_product("F", 1, 0)
                    second_product("F", 1, 1)
                if b:
                    max_transpose(0)
                if a:
                    pe.wait_ge(xnT_lo_done, st.count("A", 1, 1))
                    if st.k == LAG["A"]:
                        pe.wait_ge(w_split, 1)
                    project("q", "wq", xnT_hi, xnT_lo, q_mm)
                if g:
                    transposes("G", "x2T", x2n, x2n_done, x2T_mm)
                if a:
                    pe.wait_ge(ctx_lo_done, st.count("A", 1, 1))
                    if st.k == LAG["A"]:
                        pe.wait_ge(w_split, 2)
                    project("k", "wk", ctx_hi, ctx_lo, k_mm)
                if b:
                    shifted_scores(0)
                if g:
                    if st.k == LAG["G"]:
                        pe.wait_ge(w_split, 6)
                    first_product(0)
                    first_product(1)
                if b:
                    plain_scores(1)
                    attend("B", 0)
                if g:
                    first_product(2)
                    first_product(3)
                if b:
                    max_transpose(1)
                if a:
                    if st.k == LAG["A"]:
                        pe.wait_ge(w_split, 3)
                    rows_out("v", (ctx_hi, ctx_lo), "wv", v_mm)
                if g:
                    second_product("G", 0, 0)
                if c:
                    if st.k == LAG["C"]:
                        pe.wait_ge(w_split, 4)
                    pe.wait_ge(attn_split, st.count("C", 2, 2))
                    rows_out("o", (attn_hi, attn_lo), "wo", o_mm)
                if b:
                    shifted_scores(1)
                if g:
                    second_product("G", 0, 1)

            over_steps(pe, run_step)


_INS = ["x", "ctx_t", "mask", "wq", "wk", "wv", "wo", "w1", "w2", "bq", "bk", "bv", "bo", "b1", "b2"]


def kernel(**inputs):
    import concourse.bacc as bacc
    from concourse.bass_utils import run_bass_kernel_spmd

    n = {k.replace("L0_xattn_", "").replace("L0_ffn_", ""): np.asarray(v) for k, v in inputs.items()}

    def tiles(w):
        return w.reshape(w.shape[0] // P, P, w.shape[1]).transpose(1, 0, 2).reshape(P, -1)

    def by_dim(w):
        return w.reshape(w.shape[0], HH, KT, D).transpose(0, 2, 3, 1).reshape(w.shape[0], E)

    wo = n["Wo"].reshape(2, KT, 4, D, E).transpose(1, 2, 3, 0, 4).reshape(E, E)
    arrays = {
        "x": n["x"],
        "ctx_t": n["ctx_1024"].reshape(GROUPS, GB, S, KT, P).transpose(0, 4, 3, 1, 2).reshape(GROUPS, P, KT, T),
        "mask": n["mask_Bx1x1xS2_if1"],
        "wq": tiles(by_dim(n["Wq"])), "wk": tiles(by_dim(n["Wk"])), "wv": tiles(n["Wv"]), "wo": tiles(wo),
        "w1": tiles(n["W1"]), "w2": tiles(n["W2"]),
        "bq": by_dim(n["bq"][None]).reshape(KT, P).T, "bk": by_dim(n["bk"][None]).reshape(KT, P).T,
        "bv": n["bv"][None], "bo": n["bo"][None], "b1": n["b1"].reshape(FT, P).T, "b2": n["b2"][None],
    }
    arrays = {k: np.ascontiguousarray(v) for k, v in arrays.items()}
    nc = bacc.Bacc("TRN2", target_bir_lowering=False, num_devices=1)
    args = [nc.dram_tensor(f"in_{k}", arrays[k].shape, mybir.dt.from_np(arrays[k].dtype), kind="ExternalInput").ap()
            for k in _INS]
    out = nc.dram_tensor("out", (B, S, E), mybir.dt.float32, kind="ExternalOutput").ap()
    build(nc, *args, out)
    r = run_bass_kernel_spmd(nc, [{f"in_{k}": arrays[k] for k in _INS}], core_ids=[0])
    return r.results[0]["out"]
```
